# Optimizing a Trainium2 kernel written in Bass

```python
import numpy as np
import jax
import jax.numpy as jnp

def _softmax(x, axis=-1):
    return jax.nn.softmax(x, axis=axis)

def _gelu(x):
    return jax.nn.gelu(x, approximate=True)

def _silu(x):
    return jax.nn.silu(x)

def _sigmoid(x):
    return jax.nn.sigmoid(x)

def _layernorm(x, axis=-1, eps=1e-05):
    m = jnp.mean(x, axis=axis, keepdims=True)
    v = jnp.var(x, axis=axis, keepdims=True)
    return (x - m) / jnp.sqrt(v + eps)

def _scatter_add(tgt, idx, src, axis=0):
    return tgt.at[idx].add(src)

def _segment_sum(src, seg, n):
    return jax.ops.segment_sum(src, seg, n)
kernel_name = 'mk_seq_postln_d1_jaxref_r8_9bd547'

def setup_inputs(seed: int=0):
    np.random.seed(seed)
    _w = jnp.asarray

    def _L0_attn_setup():
        import jax, jax.numpy as jnp
        import numpy as np
        D_K, D_MODEL, NUM_HEADS = (64, 128, 16)

        def _xavier(key, shape):
            fan_in, fan_out = (shape[-2], shape[-1])
            limit = float(np.sqrt(6.0 / (fan_in + fan_out)))
            return jax.random.uniform(key, shape, jnp.float32, -limit, limit)
        key = jax.random.key(seed)
        kx, kq, kk, kv, ko = jax.random.split(key, 5)
        x = jax.random.normal(kx, (2, 256, D_MODEL), dtype=jnp.float32)
        w_q = _xavier(kq, (NUM_HEADS, D_MODEL, D_K))
        w_k = _xavier(kk, (NUM_HEADS, D_MODEL, D_K))
        w_v = _xavier(kv, (NUM_HEADS, D_MODEL, D_K))
        w_o = _xavier(ko, (NUM_HEADS * D_K, D_MODEL))
        return {'x': x, 'w_q': w_q, 'w_k': w_k, 'w_v': w_v, 'w_o': w_o}
    _L0_attn_in = _L0_attn_setup()

    def _L0_ffn_setup():
        import jax, jax.numpy as jnp
        import numpy as np
        D_MODEL, D_FF, N_EXPERTS, TOP_K = (128, 256, 8, 2)
        B, S = (2, 256)
        key = jax.random.key(seed)
        k1, k2, k3, k4 = jax.random.split(key, 4)
        scale = 0.02
        return {'x': jax.random.normal(k1, (B, S, D_MODEL), dtype=jnp.float32), 'gate_w': jax.random.normal(k2, (D_MODEL, N_EXPERTS), dtype=jnp.float32) * scale, 'w1': jax.random.normal(k3, (N_EXPERTS, D_MODEL, D_FF), dtype=jnp.float32) * scale, 'w2': jax.random.normal(k4, (N_EXPERTS, D_FF, D_MODEL), dtype=jnp.float32) * scale}
    _L0_ffn_in = _L0_ffn_setup()
    _d = {'L0_attn_x': _L0_attn_in['x'], 'L0_attn_w_q': _L0_attn_in['w_q'], 'L0_attn_w_k': _L0_attn_in['w_k'], 'L0_attn_w_v': _L0_attn_in['w_v'], 'L0_attn_w_o': _L0_attn_in['w_o'], 'L0_ffn_gate_w': _L0_ffn_in['gate_w'], 'L0_ffn_w1': _L0_ffn_in['w1'], 'L0_ffn_w2': _L0_ffn_in['w2']}
    _x0 = _d['L0_attn_x']
    _d['L0_attn_x'] = jax.random.normal(jax.random.fold_in(jax.random.key(seed), 1), (8, 512, 128), dtype=_x0.dtype)
    del _x0
    return _d

def reference(L0_attn_x, L0_attn_w_q, L0_attn_w_k, L0_attn_w_v, L0_attn_w_o, L0_ffn_gate_w, L0_ffn_w1, L0_ffn_w2):

    def _L0_attn_ref(x, w_q, w_k, w_v, w_o):
        import jax, jax.numpy as jnp
        import numpy as np
        D_K, D_MODEL, NUM_HEADS = (64, 128, 16)

        def _xavier(key, shape):
            fan_in, fan_out = (shape[-2], shape[-1])
            limit = float(np.sqrt(6.0 / (fan_in + fan_out)))
            return jax.random.uniform(key, shape, jnp.float32, -limit, limit)
        scale = 1.0 / jnp.sqrt(jnp.asarray(D_K, dtype=jnp.float32))
        q = jnp.einsum('bsd,hdk->bhsk', x, w_q)
        k = jnp.einsum('bsd,hdk->bhsk', x, w_k)
        v = jnp.einsum('bsd,hdk->bhsk', x, w_v)
        scores = jnp.einsum('bhqk,bhmk->bhqm', q, k) * scale
        weights = jax.nn.softmax(scores, axis=-1)
        z = jnp.einsum('bhqm,bhmk->bhqk', weights, v)
        b, h, s, dk = z.shape
        z = jnp.transpose(z, (0, 2, 1, 3)).reshape(b, s, h * dk)
        z = jnp.einsum('bse,ed->bsd', z, w_o)
        return x + z

    def _L0_ffn_ref(x, gate_w, w1, w2):
        import jax, jax.numpy as jnp
        import numpy as np
        D_MODEL, D_FF, N_EXPERTS, TOP_K = (128, 256, 8, 2)
        B, S = (2, 256)
        router_logits = jnp.einsum('bsd,de->bse', x, gate_w)
        top_logits, top_idx = jax.lax.top_k(router_logits, TOP_K)
        top_w = jax.nn.softmax(top_logits, axis=-1)
        combine = jnp.sum(jax.nn.one_hot(top_idx, N_EXPERTS, dtype=x.dtype) * top_w[..., None], axis=-2)
        h = jax.nn.silu(jnp.einsum('bsd,edf->ebsf', x, w1))
        y = jnp.einsum('ebsf,efd->ebsd', h, w2)
        out = jnp.einsum('ebsd,bse->bsd', y, combine)
        return out
    x = L0_attn_x
    x = _layernorm(x + _L0_attn_ref(x, L0_attn_w_q, L0_attn_w_k, L0_attn_w_v, L0_attn_w_o), axis=-1)
    x = _layernorm(x + _L0_ffn_ref(x, L0_ffn_gate_w, L0_ffn_w1, L0_ffn_w2), axis=-1)
    return x

_drawn_inputs = setup_inputs


def setup_inputs(seed=0):
    import zlib

    import numpy as np

    out = dict(_drawn_inputs(seed))
    spreads = {}
    factors = {}
    for name, (base, spread) in spreads.items():
        noise = np.random.default_rng([zlib.crc32(name.encode()), seed]).standard_normal(out[name].shape)
        drawn = base * np.exp(spread * noise) if base else spread * noise
        out[name] = jnp.asarray(drawn.astype(out[name].dtype))
    for name, factor in factors.items():
        out[name] = (out[name] * factor).astype(out[name].dtype)
    return out
```

```python
from contextlib import ExitStack

import concourse.bass as bass
from concourse import mybir

F32 = mybir.dt.float32
F32R = mybir.dt.float32r
ALU = mybir.AluOpType
ACT = mybir.ActivationFunctionType
AX = mybir.AxisListType

P = 128


def attention_moe_kernel(nc, x, w_q, w_k, w_v, w_o, gate_w, w1, w2, out):
    B, S, D = x.shape
    H, _, DK = w_q.shape
    NE, _, F = w1.shape
    HP = H // 2
    PAIRS = B * HP
    TT = S // P
    NT = B * TT
    FC = F // P
    VW = DK + 1
    SCALE = 1.0 / DK ** 0.5
    EPS = 1e-5
    STEPS = NE * B
    DMA = 16
    STACK = 4 * DMA
    assert D == P and 2 * DK == P and S == 512 and HP == B and F == 2 * P

    with ExitStack() as ctx:
        def sb(name, shape, dt=F32):
            return ctx.enter_context(nc.sbuf_tensor(name, shape, dt))

        def sem(name):
            return ctx.enter_context(nc.semaphore(name))

        x_tok = sb("x_tok", [P, NT, D])
        acc = sb("acc", [P, B, S])
        xT = sb("xT", [P, B, 2, S], F32R)
        w_tab = sb("w_tab", [P, HP, 4, 2, P], F32R)
        ident = sb("ident", [P, P])
        w1_tab = sb("w1_tab", [P, NE, 2, F], F32R)
        w2_tab = sb("w2_tab", [P, NE, FC, 2, D], F32R)
        gate_tab = sb("gate_tab", [P, 2, P], F32R)
        gate_raw = sb("gate_raw", [P, NE])
        before = sb("before", [P, NE, NE])
        exponent = sb("exponent", [P, 1])
        w_raw = acc[:].rearrange("p b s -> p (b s)").rearrange("p (w n) -> p w n", w=4)
        w1_raw = x_tok[:, 0:NT // 2, :].rearrange("p t d -> p (t d)").rearrange("p (e f) -> p e f", e=NE)
        w2_raw = x_tok[:, NT // 2:NT, :].rearrange("p t d -> p (t d)").rearrange("p (e c d) -> p e c d", e=NE, c=FC)
        wqk_cur = [sb(f"wqk_cur{j}", [P, 2, 2, P], F32R) for j in range(2)]
        wv_cur = sb("wv_cur", [P, 2, P], F32R)
        wo_cur = sb("wo_cur", [P, 2, P], F32R)
        xT_cur = sb("xT_cur", [P, 2, S], F32R)
        q_pair, k_pair = (sb(n, [P, 2, S], F32R) for n in ("q_pair", "k_pair"))
        q_stack = [sb(f"q_stack{j}", [P, 2, 2, S], F32R) for j in range(2)]
        k_stack = [sb(f"k_stack{j}", [P, 2, 2, S], F32R) for j in range(2)]
        v1 = [sb(f"v1{j}", [P, TT, 2, VW]) for j in range(2)]
        probs = [sb(f"probs{h}", [P, TT, S]) for h in range(2)]
        neg_max = [sb(f"neg_max{h}", [P, TT], F32R) for h in range(2)]
        max_row = [sb(f"max_row{h}", [TT, P]) for h in range(2)]
        r_sum = sb("r_sum", [P, TT])
        z_tok = sb("z_tok", [P, TT, P])
        zT_hi, zT_lo = (sb(n, [P, S], F32R) for n in ("zT_hi", "zT_lo"))

        psum = ctx.enter_context(nc.psum_tensor("psum", [P, 8, 512], F32))
        COARSE, MISC, Z = 4, 6, 7

        g_hi = [q_stack[j][:, 0] for j in range(2)]
        g_lo = [q_stack[j][:, 1] for j in range(2)]
        silu = [probs[0][:, FC * j:FC * (j + 1), :] for j in range(2)]
        gated = [probs[1][:, FC * j:FC * (j + 1), :] for j in range(2)]
        cT = xT_cur
        CLO = 32
        select_e = k_pair[:].rearrange("p a s -> p (a s)").rearrange("p (e m) -> p e m", e=NE)
        x1_tok = z_tok
        logitT = v1[0][:].rearrange("p t h v -> p (t h v)")[:, 0:S]
        sumT = v1[1][:].rearrange("p t h v -> p (t h v)")[:, 0:S]
        x_flat, carved = x_tok[:].rearrange("p t d -> p (t d)"), [0]

        def carve(*shape):
            n = 1
            for d in shape:
                n *= d
            ap = x_flat[:, carved[0]:carved[0] + n]
            carved[0] += n
            names = " ".join("abc"[:len(shape)])
            return ap.rearrange(f"p ({names}) -> p {names}", **dict(zip("abc", shape))) if len(shape) > 1 else ap

        select_raw = carve(NE, P)
        accT_cur = carve(S)
        out_tok = carve(TT, D)
        stats, stats2 = carve(TT, 6), carve(TT, 6)
        mv, mv2 = carve(TT, 2), carve(TT, 2)
        veps, veps2, rstd, rstd2, top, wsum, rwsum = (carve(TT) for _ in range(7))
        logit, shifted, expl, chosen, weight, combine = (carve(TT, NE) for _ in range(6))
        above, tied = carve(TT, NE, NE), carve(TT, NE, NE)
        CB, Y, NA, NB = 4, 5, 6, 7

        names = """x_in w_in ident_set ones_set zeroed w_split gate_split
            xT_done xT_hi_done xT_lo_done acc_set
            wv_cur_in wo_cur_in xT_cur_in
            q_done k_done vT_done q_hi_done q_lo_done k_hi_done k_lo_done v_done
            coarse_done max_done maxT_done max_row_done
            scores_done exp_done pv_done z_done r_done
            zT_done zT_hi_done zT_lo_done wo_done acc_done
            experts_in x_out xt_cleared gate_in gate_set experts_hi experts_split sel_set const_set
            accT_in tok_done mv_done rstd_done x1_done x1T_done x1T_hi_done x1T_lo_done
            logitT_done logitT_out logit_done logit_out shifted route_step exp_logit c_done cT_done cT_hi_done cT_lo_done
            h_done cb_done silu_done gated g_hi_done g_lo_done y_done
            sum_half sum_done sum_tok_done mv2_done rstd2_done stats_done stats2_done norm2_done""".split()
        s = {n: sem(n) for n in names}
        q_stacked = [sem(f"q_stacked{j}") for j in range(2)]
        k_stacked = [sem(f"k_stacked{j}") for j in range(2)]
        wqk_cur_in = [sem(f"wqk_cur_in{j}") for j in range(2)]
        shift_in = [sem(f"shift_in{h}") for h in range(2)]
        w_sem = [sem(f"w_in{k}") for k in range(4)]

        def wait(eng, semaphore, value):
            if not isinstance(value, int) or value > 0:
                eng.wait_ge(semaphore, value)

        def wait_apart(eng, *pairs):
            pairs = [(semaphore, v if isinstance(v, int) else eng.to_reg(v)) for semaphore, v in pairs]
            if not all(isinstance(v, int) for _, v in pairs):
                eng.wait_ge(s["ident_set"], 1)
            for semaphore, v in pairs:
                wait(eng, semaphore, v)

        def bits(ap):
            return ap.bitcast(F32)

        def loops(eng, body):
            body(0, 0)
            body(1, 1)
            with eng.Fori(1, PAIRS // 2 - 1) as i:
                body(i * 2, 0)
                body(i * 2 + 1, 1)
            body(PAIRS - 2, 0)
            body(PAIRS - 1, 1)

        def chunks(eng, body):
            body(0, 0)
            body(1, 1)
            with eng.Fori(1, B // 2 - 1) as i:
                body(i * 2, 0)
                body(i * 2 + 1, 1)
            body(B - 2, 0)
            body(B - 1, 1)

        def is_first(n):
            return isinstance(n, int) and n == 0

        def last_step(b, ahead):
            return isinstance(b, int) and b == B - 1 and ahead >= NE

        def is_last(n, ahead):
            return isinstance(n, int) and n + ahead >= PAIRS

        x_dram = x.rearrange("b (t p) d -> p (b t) d", p=P)
        w1_dram = w1.rearrange("e d f -> d e f")
        w2_dram = w2.rearrange("e (c p) d -> p e c d", p=P)
        w_dram = [w.rearrange("h d k -> d h k") for w in (w_q, w_k, w_v)]
        out_dram = out.rearrange("b (t p) d -> p (b t) d", p=P)

        block = ctx.enter_context(nc.Block())

        @block.sync
        def _(sp):
            for k in range(3):
                sp.dma_start(w_raw[:, k, :].rearrange("p (h k) -> p h k", h=H), w_dram[k]).then_inc(w_sem[k], DMA)
            for b in range(B):
                sp.dma_start(x_tok[:, b * TT:(b + 1) * TT, :], x_dram[:, b * TT:(b + 1) * TT, :]).then_inc(s["x_in"], DMA)
                if b == 0:
                    sp.dma_start(w_raw[:, 3, :].rearrange("p (c d) -> p c d", c=HP),
                                 w_o.rearrange("(c p) d -> p c d", p=P)).then_inc(w_sem[3], DMA)

            def load_wqk(m, j):
                wait_apart(sp, (s["k_done"], m - 1))
                sp.dma_start(bits(wqk_cur[j][:]), bits(w_tab[:, m % HP, 0:2])).then_inc(wqk_cur_in[j], DMA)

            def load_wv(m):
                wait_apart(sp, (s["vT_done"], m))
                sp.dma_start(bits(wv_cur[:]), bits(w_tab[:, m % HP, 2])).then_inc(s["wv_cur_in"], DMA)

            def load_xT(m):
                wait_apart(sp, (s["vT_done"], m))
                sp.dma_start(bits(xT_cur[:]), bits(xT[:, m // HP])).then_inc(s["xT_cur_in"], DMA)

            def stack_k(j, m):
                wait_apart(sp, (s["scores_done"], 4 * (m - 1)), (s["k_hi_done"], m + 1), (s["k_lo_done"], m + 1))
                for h in range(2):
                    half = slice(h * DK, (h + 1) * DK)
                    sp.dma_start(bits(k_stack[j][0:DK, h]),
                                 bits(k_pair[half, 0:1]).broadcast_to([DK, 2, S])).then_inc(k_stacked[j], DMA)
                    sp.dma_start(bits(k_stack[j][DK:P, h, 0]), bits(k_pair[half, 1])).then_inc(k_stacked[j], DMA)

            def load_shift(j, h, k):
                wait(sp, s["max_row_done"], k + 1)
                sp.dma_start(bits(q_stack[j][DK:VW, h, 1, :]), max_row[h][:]).then_inc(shift_in[h], DMA)

            sp.wait_ge(s["w_split"], 4)
            sp.wait_ge(s["xT_hi_done"], 1)
            sp.wait_ge(s["xT_lo_done"], 1)
            load_wqk(0, 0)
            load_wqk(1, 1)
            load_xT(0)
            load_wv(0)
            stack_k(0, 0)
            stack_k(1, 1)
            load_shift(0, 0, 0)
            sp.wait_ge(s["xT_hi_done"], B)
            sp.wait_ge(s["xT_lo_done"], B)

            def body(n, j):
                if not is_last(n, 2):
                    load_wqk(n + 2, j)
                if not is_last(n, 1):
                    load_wv(n + 1)
                    if j == 1:
                        load_xT(n + 1)
                if not is_first(n):
                    wait_apart(sp, (s["wo_done"], n - 1))
                    sp.dma_start(bits(wo_cur[:]), bits(w_tab[:, (n - 1) % HP, 3])).then_inc(s["wo_cur_in"], DMA)
                load_shift(j, 1, 2 * n + 1)
                if not is_last(n, 1):
                    load_shift(1 - j, 0, 2 * n + 2)
                if not is_last(n, 2):
                    stack_k(j, n + 2)

            sp.wait_ge(s["xT_done"], B)
            sp.dma_start(w1_raw, w1_dram).then_inc(s["experts_in"], DMA)
            sp.dma_start(w2_raw, w2_dram).then_inc(s["experts_in"], DMA)
            sp.dma_start(gate_raw[:], gate_w).then_inc(s["gate_in"], DMA)

            loops(sp, body)
            sp.wait_ge(s["wo_done"], PAIRS - 1)
            sp.dma_start(bits(wo_cur[:]), bits(w_tab[:, HP - 1, 3])).then_inc(s["wo_cur_in"], DMA)

            def load_accT(b):
                wait_apart(sp, (s["tok_done"], b))
                sp.dma_start(accT_cur[:], acc[:, b, :]).then_inc(s["accT_in"], DMA)

            def store(b):
                wait_apart(sp, (s["norm2_done"], TT * (b + 1)))
                sp.dma_start(out_dram[:, bass.ds(b * TT, TT), :], out_tok).then_inc(s["x_out"], DMA)

            sp.wait_ge(s["acc_done"], PAIRS)
            sp.wait_ge(s["experts_split"], 2 * NE)
            load_accT(0)

            def chunk(b, j):
                if not (isinstance(b, int) and b == B - 1):
                    load_accT(b + 1)
                if not is_first(b):
                    store(b - 1)

            chunks(sp, chunk)
            store(B - 1)
            sp.wait_ge(s["x_out"], DMA * B)

        @block.gpsimd
        def _(pool):
            nc.gpsimd.memset(ident[:], 0.0).then_inc(s["zeroed"], 1)
            pool.wait_ge(s["zeroed"], 1)
            nc.gpsimd.affine_select(out=ident[:], in_=ident[:], compare_op=ALU.not_equal, fill=1.0, base=0,
                                    pattern=[[-1, P]], channel_multiplier=1).then_inc(s["ident_set"], 1)
            pool.wait_ge(s["ident_set"], 1)
            for j in range(2):
                nc.gpsimd.memset(bits(k_stack[j][DK:VW, :, 1, :]), 1.0).then_inc(s["ones_set"], 1)
                pool.wait_ge(s["ones_set"], 2 * j + 1)
                nc.gpsimd.memset(v1[j][:, :, :, DK:VW], 1.0).then_inc(s["ones_set"], 1)
                pool.wait_ge(s["ones_set"], 2 * j + 2)
            nc.gpsimd.memset(exponent[:], -0.5).then_inc(s["const_set"], 1)
            pool.wait_ge(s["const_set"], 1)
            nc.gpsimd.memset(before[:], 0.0).then_inc(s["const_set"], 1)
            pool.wait_ge(s["const_set"], 2)
            nc.gpsimd.affine_select(out=before[:], in_=before[:], compare_op=ALU.is_ge, fill=1.0, base=0,
                                    pattern=[[-1, NE], [1, NE]], channel_multiplier=0).then_inc(s["const_set"], 1)
            pool.wait_ge(s["const_set"], 3)
            nc.gpsimd.memset(bits(gate_tab[:]), 0.0).then_inc(s["gate_set"], 1)

            def stack_q(j, m):
                wait_apart(pool, (s["scores_done"], 4 * (m - 1)), (s["q_hi_done"], m + 1), (s["q_lo_done"], m + 1))
                for h in range(2):
                    half = slice(h * DK, (h + 1) * DK)
                    pool.dma_start(bits(q_stack[j][0:DK, h]), bits(q_pair[half])).then_inc(q_stacked[j], DMA)
                    pool.dma_start(bits(q_stack[j][DK:P, h, 0]), bits(q_pair[half, 0])).then_inc(q_stacked[j], DMA)

            for m in range(2):
                stack_q(m, m)

            def body(n, j):
                if not is_last(n, 2):
                    stack_q(j, n + 2)

            def split_experts():
                pool.wait_ge(s["experts_in"], 2 * DMA)
                tables = [(w1_tab, w1_raw), (w2_tab, w2_raw)]
                n = 0
                for tab, raw in tables:
                    for e in range(NE):
                        part = (lambda q: tab[:, e, q]) if tab is w1_tab else (lambda q: tab[:, e, :, q])
                        nc.gpsimd.tensor_scalar(part(0), raw[:, e], 1.0, 0.0, ALU.mult, ALU.add).then_inc(s["experts_hi"], 1)
                        n += 1
                        pool.wait_ge(s["experts_hi"], n)
                        nc.gpsimd.tensor_tensor(part(1), raw[:, e], bits(part(0)), ALU.subtract).then_inc(s["experts_split"], 1)

            split_experts()
            loops(pool, body)

            def rstd_part(sem_in, sem_out, mvs, v, r, b):
                wait_apart(pool, (s[sem_in], TT * (b + 1)))
                nc.gpsimd.tensor_scalar(v[:], mvs[:, :, 1], 1.0, EPS, ALU.mult, ALU.add).then_inc(s[sem_out], 1)
                pool.wait_ge(s[sem_out], 2 * b + 1)
                nc.gpsimd.tensor_tensor(r[:], v[:], exponent[:].broadcast_to([P, TT]), ALU.pow).then_inc(s[sem_out], 1)

            def g_lo_part(k, e):
                pool.wait_ge(s["g_hi_done"], k + 1)
                nc.gpsimd.tensor_tensor(g_lo[e % 2], gated[e % 2], bits(g_hi[e % 2]), ALU.subtract).then_inc(s["g_lo_done"], 1)

            pool.wait_ge(s["experts_split"], 2 * NE)
            nc.gpsimd.memset(select_raw, 0.0).then_inc(s["sel_set"], 1)
            pool.wait_ge(s["sel_set"], 1)
            for i, first in enumerate((0, CLO)):
                nc.gpsimd.affine_select(out=select_raw, in_=select_raw, compare_op=ALU.not_equal, fill=1.0,
                                        base=-first, pattern=[[-1, NE], [0, P]], channel_multiplier=1).then_inc(s["sel_set"], 1)
                pool.wait_ge(s["sel_set"], i + 2)
            pool.wait_ge(s["pv_done"], 2 * PAIRS)
            nc.gpsimd.tensor_scalar(select_e, select_raw, 1.0, 0.0, ALU.mult, ALU.add).then_inc(s["sel_set"], 1)
            nc.gpsimd.memset(bits(cT[:]), 0.0).then_inc(s["xt_cleared"], 1)
            rstd_part("mv_done", "rstd_done", mv, veps, rstd, 0)
            g_lo_part(0, 0)

            def chunk(b, j):
                for e in range(NE):
                    if not last_step(b, e + 1):
                        g_lo_part(b * NE + e + 1, e + 1)
                    if e == 0 and not last_step(b, NE):
                        rstd_part("mv_done", "rstd_done", mv, veps, rstd, b + 1)
                    if e == 1 and not is_first(b):
                        rstd_part("mv2_done", "rstd2_done", mv2, veps2, rstd2, b - 1)

            chunks(pool, chunk)
            rstd_part("mv2_done", "rstd2_done", mv2, veps2, rstd2, B - 1)

        @block.tensor
        def _(pe):
            pe.wait_ge(s["ident_set"], 1)
            pe.wait_ge(s["x_in"], DMA * B)
            for b in range(B):
                wait(pe, s["xT_hi_done"], b - 3)
                wait(pe, s["xT_lo_done"], b - 3)
                wait(pe, s["acc_set"], b - 3)
                for t in range(TT):
                    mm = nc.tensor.transpose(psum[:, b % 4, t * P:(t + 1) * P], x_tok[:, b * TT + t, :], ident[:])
                mm.then_inc(s["xT_done"], 1)

            def product(dst, left, right, start=True, stop=True):
                (lh, ll), (rh, rl) = left, right
                nc.tensor.matmul(dst, lh, rh, start=start, stop=False)
                nc.tensor.matmul(dst, lh, rl, start=False, stop=False)
                return nc.tensor.matmul(dst, ll, rh, start=False, stop=stop)

            def project_qk(which, m, j):
                w = [wqk_cur[j][:, which, part, :] for part in range(2)]
                return product(psum[:, MISC, :], w, [xT[:, m // HP, part, :] for part in range(2)])

            def project_q(m, i, j):
                pe.wait_ge(wqk_cur_in[j], DMA * (i + 1))
                wait(pe, s["k_hi_done"], m)
                wait(pe, s["k_lo_done"], m)
                wait(pe, s["v_done"], m - 1)
                wait(pe, s["acc_done"], m - 3)
                project_qk(0, m, j).then_inc(s["q_done"], 1)

            def project_k(m, j):
                pe.wait_ge(s["q_hi_done"], m + 1)
                pe.wait_ge(s["q_lo_done"], m + 1)
                project_qk(1, m, j).then_inc(s["k_done"], 1)

            def project_v(m, loads):
                pe.wait_ge(s["wv_cur_in"], DMA * (m + 1))
                pe.wait_ge(s["xT_cur_in"], DMA * loads)
                wait(pe, s["k_hi_done"], m + 2 if not is_last(m, 1) else PAIRS)
                wait(pe, s["k_lo_done"], m + 2 if not is_last(m, 1) else PAIRS)
                wait(pe, s["zT_hi_done"], m - 1)
                wait(pe, s["zT_lo_done"], m - 1)
                for t in range(TT):
                    tok = slice(t * P, (t + 1) * P)
                    mm = product(psum[:, MISC, tok], [xT_cur[:, 0, tok], xT_cur[:, 1, tok]],
                                 [wv_cur[:, 0, :], wv_cur[:, 1, :]])
                mm.then_inc(s["vT_done"], 1)

            def coarse(n, i, j, h, t):
                k = 2 * n + h
                if t == 0 and h == 0:
                    pe.wait_ge(q_stacked[j], STACK * (i + 1))
                    pe.wait_ge(k_stacked[j], STACK * (i + 1))
                wait(pe, s["max_done"], TT * k + t - 1)
                nc.tensor.matmul(psum[:, COARSE + t % 2, :], q_stack[j][:, h, 0, t * P:(t + 1) * P], k_stack[j][:, h, 0, :],
                                 start=True, stop=True).then_inc(s["coarse_done"], 1)

            def shift_rows(n, h):
                k = 2 * n + h
                pe.wait_ge(s["max_done"], TT * (k + 1))
                wait(pe, s["z_done"], k - 2)
                wait(pe, s["max_row_done"], k)
                nc.tensor.transpose(psum[0:TT, Z, 384:512], bits(neg_max[h][:]), ident[:]).then_inc(s["maxT_done"], 1)

            def scores(n, j, h):
                k = 2 * n + h
                pe.wait_ge(shift_in[h], DMA * (n + 1))
                for g in range(2):
                    wait(pe, s["exp_done"], 2 * (k - 1) + g + 1)
                    for t in range(2 * g, 2 * g + 2):
                        keys = slice(t * P, (t + 1) * P)
                        nc.tensor.matmul(psum[:, t, :], k_stack[j][:, h, 0, keys], q_stack[j][:, h, 0, :], start=True, stop=False)
                        mm = nc.tensor.matmul(psum[:, t, :], k_stack[j][0:VW, h, 1, keys], q_stack[j][0:VW, h, 1, :], start=False, stop=True)
                    mm.then_inc(s["scores_done"], 1)

            def times_v(n, j, h, t, rows_follow=None):
                k = 2 * n + h
                if t == 0:
                    wait(pe, s["z_done"], k)
                    pe.wait_ge(s["v_done"], n + 1)
                    pe.wait_ge(s["exp_done"], 2 * k + 2)
                    pe.wait_ge(s["max_row_done"], 2 * PAIRS if rows_follow is False else k + 3)
                for c in range(TT):
                    mm = nc.tensor.matmul(psum[:, Z, t * VW:(t + 1) * VW], probs[h][:, c, t * P:(t + 1) * P],
                                          v1[j][:, c, h, :], start=(c == 0), stop=(c == TT - 1))
                if t == TT - 1:
                    mm.then_inc(s["pv_done"], 1)

            def transpose_z(n):
                pe.wait_ge(s["z_done"], 2 * n + 2)
                wait(pe, s["k_hi_done"], n + 4 if not is_last(n, 3) else PAIRS)
                wait(pe, s["k_lo_done"], n + 4 if not is_last(n, 3) else PAIRS)
                wait(pe, s["acc_done"], n)
                for t in range(TT):
                    mm = nc.tensor.transpose(psum[:, MISC, t * P:(t + 1) * P], z_tok[:, t, :], ident[:])
                mm.then_inc(s["zT_done"], 1)

            def project_out(n):
                pe.wait_ge(s["zT_hi_done"], n + 1)
                pe.wait_ge(s["zT_lo_done"], n + 1)
                pe.wait_ge(s["wo_cur_in"], DMA * (n + 1))
                pe.wait_ge(s["v_done"], n + 3 if not is_last(n, 2) else PAIRS)
                mm = product(psum[:, MISC, :], [wo_cur[:, 0, :], wo_cur[:, 1, :]], [zT_hi[:], zT_lo[:]])
                mm.then_inc(s["wo_done"], 1)

            for m in range(2):
                project_q(m, 0, m)
                project_k(m, m)
            project_v(0, 1)
            pe.wait_ge(s["ones_set"], 4)
            for h in range(2):
                for t in range(TT):
                    coarse(0, 0, 0, h, t)
                if h == 0:
                    shift_rows(0, 0)

            def body(n, j):
                ahead, project = not is_last(n, 1), not is_last(n, 2)

                def turn(m, parity):
                    return (m - parity) // 2

                early = [(0, 1), (2,), (3,), ()]
                scores(n, j, 0)
                shift_rows(n, 1)
                if project:
                    project_q(n + 2, turn(n + 2, j), j)
                for t in range(TT):
                    for u in early[t] if ahead else ():
                        coarse(n + 1, turn(n + 1, 1 - j), 1 - j, 0, u)
                    if not is_first(n):
                        times_v(n - 1, 1 - j, 1, t, rows_follow=False if is_last(n, 1) else None)
                if project:
                    project_k(n + 2, j)
                scores(n, j, 1)
                if ahead:
                    shift_rows(n + 1, 0)
                if not is_first(n):
                    transpose_z(n - 1)
                for t in range(TT):
                    for u in early[t] if ahead else ():
                        coarse(n + 1, turn(n + 1, 1 - j), 1 - j, 1, u)
                    if t == 2 and ahead:
                        project_v(n + 1, turn(n + 1, 1 - j) + 1 if j == 1 else turn(n, j) + 1)
                    times_v(n, j, 0, t, rows_follow=False if is_last(n, 1) else None)
                if not is_first(n):
                    project_out(n - 1)

            loops(pe, body)
            for t in range(TT):
                times_v(PAIRS - 1, 1, 1, t, rows_follow=False)
            transpose_z(PAIRS - 1)
            project_out(PAIRS - 1)

            def to_tokens(b):
                pe.wait_ge(s["accT_in"], DMA * (b + 1))
                wait(pe, s["cT_hi_done"], b)
                wait(pe, s["cT_lo_done"], b)
                for t in range(TT):
                    mm = nc.tensor.transpose(psum[:, NA, t * P:(t + 1) * P], accT_cur[:, t * P:(t + 1) * P], ident[:])
                mm.then_inc(s["tok_done"], 1)

            def transpose_x1(b):
                pe.wait_ge(s["x1_done"], TT * (b + 1))
                for t in range(TT):
                    mm = nc.tensor.transpose(psum[:, NA, t * P:(t + 1) * P], x1_tok[:, t, :], ident[:])
                mm.then_inc(s["x1T_done"], 1)

            def route(b):
                pe.wait_ge(s["x1T_hi_done"], b + 1)
                pe.wait_ge(s["x1T_lo_done"], b + 1)
                wait(pe, s["norm2_done"], TT * (b - 1))
                product(psum[:, NB, :], [gate_tab[:, 0, :], gate_tab[:, 1, :]],
                        [xT[:, b, 0, :], xT[:, b, 1, :]]).then_inc(s["logitT_done"], 1)

            def logits_to_tokens(b):
                pe.wait_ge(s["logitT_out"], b + 1)
                for t in range(TT):
                    mm = nc.tensor.transpose(psum[:, NB, t * P:(t + 1) * P], logitT[:, t * P:(t + 1) * P], ident[:])
                mm.then_inc(s["logit_done"], 1)

            def transpose_c(b):
                pe.wait_ge(s["c_done"], b + 1)
                for t in range(TT):
                    mm = nc.tensor.transpose(psum[0:NE, NA, t * P:(t + 1) * P], combine[:, t, :], ident[:])
                mm.then_inc(s["cT_done"], 1)

            def hidden(k, b, e):
                wait(pe, s["silu_done"], k - 1)
                for f in range(FC):
                    cols = slice(f * P, (f + 1) * P)
                    mm = product(psum[:, FC * (e % 2) + f, :], [w1_tab[:, e, 0, cols], w1_tab[:, e, 1, cols]],
                                 [xT[:, b, 0, :], xT[:, b, 1, :]])
                mm.then_inc(s["h_done"], 1)

            def spread_c(k, b, j, e):
                if e == 0:
                    pe.wait_ge(s["cT_hi_done"], b + 1)
                    pe.wait_ge(s["cT_lo_done"], b + 1)
                wait(pe, s["gated"], k)
                nc.tensor.matmul(psum[:, CB, :], select_e[:, e, :], cT[:, j, :], start=True,
                                 stop=True).then_inc(s["cb_done"], 1)

            def second(k, b, e):
                if e == 0:
                    wait(pe, s["sum_half"], b)
                pe.wait_ge(s["g_hi_done"], k + 1)
                for f in range(FC):
                    for part in range(2):
                        nc.tensor.matmul(psum[:, Y, :], w2_tab[:, e, f, part, :], g_hi[e % 2][:, f, :],
                                         start=(e == 0 and f == 0 and part == 0), stop=False)
                pe.wait_ge(s["g_lo_done"], k + 1)
                for f in range(FC):
                    mm = nc.tensor.matmul(psum[:, Y, :], w2_tab[:, e, f, 0, :], g_lo[e % 2][:, f, :],
                                          start=False, stop=(e == NE - 1 and f == FC - 1))
                mm.then_inc(s["y_done"], 1)

            def sum_to_tokens(b):
                pe.wait_ge(s["sum_done"], b + 1)
                wait(pe, s["logit_out"], b + 2 if not (isinstance(b, int) and b == B - 1) else B)
                for t in range(TT):
                    mm = nc.tensor.transpose(psum[:, NB, t * P:(t + 1) * P], sumT[:, t * P:(t + 1) * P], ident[:])
                mm.then_inc(s["sum_tok_done"], 1)

            pe.wait_ge(s["gate_set"], 3)
            pe.wait_ge(s["sel_set"], 4)
            pe.wait_ge(s["experts_split"], 2 * NE)
            pe.wait_ge(s["exp_done"], 4 * PAIRS)
            pe.wait_ge(s["acc_done"], PAIRS)
            to_tokens(0)
            transpose_x1(0)
            route(0)
            logits_to_tokens(0)
            transpose_c(0)
            for e in range(2):
                hidden(e, 0, e)
                spread_c(e, 0, 0, e)

            def chunk(b, j):
                nxt = not last_step(b, NE)
                for e in range(NE):
                    k = b * NE + e
                    if not last_step(b, e + 2):
                        hidden(k + 2, b + (e + 2) // NE, (e + 2) % NE)
                    if nxt:
                        if e == 0:
                            to_tokens(b + 1)
                        if e == 2:
                            transpose_x1(b + 1)
                        if e == 3:
                            route(b + 1)
                        if e == 4:
                            logits_to_tokens(b + 1)
                        if e == 5:
                            transpose_c(b + 1)
                    if e == 1 and not is_first(b):
                        sum_to_tokens(b - 1)
                    second(k, b, e)
                    if not last_step(b, e + 2):
                        spread_c(k + 2, b + (e + 2) // NE, (j + (e + 2) // NE) % 2, (e + 2) % NE)

            chunks(pe, chunk)
            sum_to_tokens(B - 1)

        @block.scalar
        def _(act):
            for k in range(4):
                act.wait_ge(w_sem[k], DMA)
                nc.scalar.activation(w_tab[:, :, k, 0, :], w_raw[:, k, :].rearrange("p (c n) -> p c n", c=HP),
                                     ACT.Copy).then_inc(s["w_in"], 1)
            for b in range(B):
                act.wait_ge(s["xT_done"], b + 1)
                nc.scalar.activation(xT[:, b, 0, :], psum[:, b % 4, :], ACT.Copy).then_inc(s["xT_hi_done"], 1)
                act.wait_ge(s["w_split"], 4)
                nc.scalar.activation(acc[:, b, :], psum[:, b % 4, :], ACT.Copy, scale=2.0).then_inc(s["acc_set"], 1)

            def q_part(n, j):
                act.wait_ge(s["q_done"], n + 1)
                free_stage(q_stacked, n, j)
                nc.scalar.activation(q_pair[:, 0, :], psum[:, MISC, :], ACT.Copy, scale=SCALE).then_inc(s["q_hi_done"], 1)

            def k_part(n, j):
                act.wait_ge(s["k_done"], n + 1)
                free_stage(k_stacked, n, j)
                nc.scalar.activation(k_pair[:, 0, :], psum[:, MISC, :], ACT.Copy).then_inc(s["k_hi_done"], 1)

            def free_stage(stacked, n, j):
                wait(act, stacked[1 - j], STACK * ((n - 1 - (1 - j)) // 2 + 1))

            def v_part(n, j):
                act.wait_ge(s["vT_done"], n + 1)
                wait(act, s["pv_done"], 2 * n - 2)
                nc.scalar.activation(v1[j][:, :, :, 0:DK], psum[:, MISC, :].rearrange("p (c h k) -> p c h k", c=TT, h=2),
                                     ACT.Copy).then_inc(s["v_done"], 1)

            def exps(n, h):
                k = 2 * n + h
                wait(act, s["pv_done"], k - 1)
                for g in range(2):
                    act.wait_ge(s["scores_done"], 2 * k + g + 1)
                    nc.scalar.activation(probs[h][:, 2 * g:2 * g + 2, :], psum[:, 2 * g:2 * g + 2, :],
                                         ACT.Exp).then_inc(s["exp_done"], 1)

            def zT_part(n):
                act.wait_ge(s["zT_done"], n + 1)
                wait(act, s["wo_done"], n)
                nc.scalar.activation(zT_hi[:], psum[:, MISC, :], ACT.Copy).then_inc(s["zT_hi_done"], 1)

            for n in range(2):
                q_part(n, n)
                k_part(n, n)
            v_part(0, 0)

            def body(n, j):
                exps(n, 0)
                if not is_last(n, 2):
                    q_part(n + 2, j)
                    k_part(n + 2, j)
                exps(n, 1)
                if not is_first(n):
                    zT_part(n - 1)
                if not is_last(n, 1):
                    v_part(n + 1, 1 - j)

            loops(act, body)
            zT_part(PAIRS - 1)

            def x1T_part(b):
                act.wait_ge(s["x1T_done"], b + 1)
                nc.scalar.activation(xT[:, b, 0, :], psum[:, NA, :], ACT.Copy).then_inc(s["x1T_hi_done"], 1)

            def logitT_part(b):
                act.wait_ge(s["logitT_done"], b + 1)
                wait(act, s["logit_done"], b)
                nc.scalar.activation(logitT, psum[:, NB, :], ACT.Copy).then_inc(s["logitT_out"], 1)

            def exp_part(b):
                act.wait_ge(s["shifted"], b + 1)
                nc.scalar.activation(expl[:], shifted[:], ACT.Exp).then_inc(s["exp_logit"], 1)

            def cT_part(b, j):
                act.wait_ge(s["cT_done"], b + 1)
                wait(act, s["cb_done"], NE * (b - 1))
                nc.scalar.activation(cT[0:NE, j, :], psum[0:NE, NA, :], ACT.Copy).then_inc(s["cT_hi_done"], 1)

            def silu_part(k, e):
                act.wait_ge(s["h_done"], k + 1)
                wait(act, s["gated"], k - 1)
                nc.scalar.activation(silu[e % 2], psum[:, FC * (e % 2):FC * (e % 2 + 1), :],
                                     ACT.Silu).then_inc(s["silu_done"], 1)

            def g_hi_part(k, e):
                act.wait_ge(s["gated"], k + 1)
                wait(act, s["y_done"], k - 1)
                nc.scalar.activation(g_hi[e % 2], gated[e % 2], ACT.Copy).then_inc(s["g_hi_done"], 1)

            x1T_part(0)
            logitT_part(0)
            exp_part(0)
            act.wait_ge(s["xt_cleared"], 1)
            cT_part(0, 0)
            silu_part(0, 0)
            g_hi_part(0, 0)
            silu_part(1, 1)

            def chunk(b, j):
                nxt = not last_step(b, NE)
                for e in range(NE):
                    k = b * NE + e
                    if not last_step(b, e + 1):
                        g_hi_part(k + 1, (e + 1) % NE)
                    if not last_step(b, e + 2):
                        silu_part(k + 2, (e + 2) % NE)
                    if nxt:
                        if e == 2:
                            x1T_part(b + 1)
                        if e == 3:
                            logitT_part(b + 1)
                        if e == 4:
                            exp_part(b + 1)
                        if e == 5:
                            cT_part(b + 1, 1 - j)

            chunks(act, chunk)

        @block.vector
        def _(dve):
            for k in range(4):
                dve.wait_ge(s["w_in"], k + 1)
                nc.vector.tensor_tensor(w_tab[:, :, k, 1, :], w_raw[:, k, :].rearrange("p (c n) -> p c n", c=HP),
                                        bits(w_tab[:, :, k, 0, :]), ALU.subtract).then_inc(s["w_split"], 1)
            for b in range(B):
                dve.wait_ge(s["acc_set"], b + 1)
                nc.vector.tensor_tensor(xT[:, b, 1, :], psum[:, b % 4, :], bits(xT[:, b, 0, :]),
                                        ALU.subtract).then_inc(s["xT_lo_done"], 1)

            def q_part(n, j):
                dve.wait_ge(s["q_hi_done"], n + 1)
                free_stage(q_stacked, n, j)
                nc.vector.scalar_tensor_tensor(q_pair[:, 1, :], psum[:, MISC, :], SCALE, bits(q_pair[:, 0, :]), ALU.mult,
                                               ALU.subtract).then_inc(s["q_lo_done"], 1)

            def k_part(n, j):
                dve.wait_ge(s["k_hi_done"], n + 1)
                free_stage(k_stacked, n, j)
                nc.vector.tensor_tensor(k_pair[:, 1, :], psum[:, MISC, :], bits(k_pair[:, 0, :]), ALU.subtract).then_inc(s["k_lo_done"], 1)

            def free_stage(stacked, n, j):
                wait(dve, stacked[1 - j], STACK * ((n - 1 - (1 - j)) // 2 + 1))

            def maxima(n, h, tiles=range(TT)):
                k = 2 * n + h
                if tiles[0] == 0:
                    wait(dve, s["maxT_done"], k - 1)
                for t in tiles:
                    dve.wait_ge(s["coarse_done"], TT * k + t + 1)
                    nc.vector.tensor_reduce(neg_max[h][:, t:t + 1], psum[:, COARSE + t % 2, :], AX.X, ALU.max,
                                            negate=True).then_inc(s["max_done"], 1)

            def shift_part(n, h):
                k = 2 * n + h
                dve.wait_ge(s["maxT_done"], k + 1)
                wait(dve, shift_in[h], DMA * n)
                nc.vector.tensor_copy(max_row[h][:], psum[0:TT, Z, 384:512]).then_inc(s["max_row_done"], 1)

            def z_part(n, h):
                k = 2 * n + h
                dve.wait_ge(s["pv_done"], k + 1)
                z = psum[:, Z, 0:TT * VW].rearrange("p (t v) -> p t v", t=TT)
                wait(dve, s["z_done"], k)
                nc.vector.reciprocal(r_sum[:].rearrange("p (t o) -> p t o", o=1), z[:, :, DK:VW]).then_inc(s["r_done"], 1)
                dve.wait_ge(s["r_done"], k + 1)
                wait(dve, s["zT_done"], n)
                nc.vector.tensor_tensor(z_tok[:, :, h * DK:(h + 1) * DK], z[:, :, 0:DK],
                                        r_sum[:].rearrange("p (t o) -> p t o", o=1).broadcast_to([P, TT, DK]),
                                        ALU.mult).then_inc(s["z_done"], 1)

            def zT_part(n):
                dve.wait_ge(s["zT_hi_done"], n + 1)
                wait(dve, s["wo_done"], n)
                nc.vector.tensor_tensor(zT_lo[:], psum[:, MISC, :], bits(zT_hi[:]), ALU.subtract).then_inc(s["zT_lo_done"], 1)

            def acc_part(n):
                dve.wait_ge(s["wo_done"], n + 1)
                wait(dve, s["acc_done"], n)
                a = acc[:, n // HP, :]
                nc.vector.tensor_tensor(a, psum[:, MISC, :], a, ALU.add).then_inc(s["acc_done"], 1)

            dve.wait_ge(s["acc_set"], B)
            for n in range(2):
                q_part(n, n)
                k_part(n, n)
            maxima(0, 0)
            shift_part(0, 0)
            maxima(0, 1)

            def body(n, j):
                ahead, project = not is_last(n, 1), not is_last(n, 2)
                shift_part(n, 1)
                if ahead:
                    maxima(n + 1, 0, (0, 1))
                if project:
                    q_part(n + 2, j)
                if ahead:
                    maxima(n + 1, 0, (2, 3))
                if not is_first(n):
                    z_part(n - 1, 1)
                if project:
                    k_part(n + 2, j)
                if ahead:
                    shift_part(n + 1, 0)
                if ahead:
                    maxima(n + 1, 1, (0, 1))
                if not is_first(n):
                    zT_part(n - 1)
                if ahead:
                    maxima(n + 1, 1, (2, 3))
                z_part(n, 0)
                if not is_first(n):
                    acc_part(n - 1)

            loops(dve, body)
            z_part(PAIRS - 1, 1)
            zT_part(PAIRS - 1)
            acc_part(PAIRS - 1)

            dve.wait_ge(s["gate_in"], DMA)
            dve.wait_ge(s["gate_set"], 1)
            nc.vector.tensor_copy(gate_tab[:, 0, 0:NE], gate_raw[:]).then_inc(s["gate_set"], 1)
            dve.wait_ge(s["gate_set"], 2)
            nc.vector.tensor_tensor(gate_tab[:, 1, 0:NE], gate_raw[:], bits(gate_tab[:, 0, 0:NE]),
                                    ALU.subtract).then_inc(s["gate_set"], 1)

            def norm_stats(bank, st, mvs, b, tok_sem, st_sem, mv_sem, free_sem):
                dve.wait_ge(s[tok_sem], b + 1)
                wait(dve, s[mv_sem], TT * b)
                for t in range(TT):
                    nc.vector.bn_stats(st[:, t], psum[:, bank, t * P:(t + 1) * P]).then_inc(s[st_sem], 1)
                wait_apart(dve, (s[st_sem], TT * (b + 1)), (s[free_sem[0]], free_sem[1] * b))
                for t in range(TT):
                    nc.vector.bn_aggr(mvs[:, t], st[:, t]).then_inc(s[mv_sem], 1)

            def stats1(b):
                norm_stats(NA, stats, mv, b, "tok_done", "stats_done", "mv_done", ("x1_done", TT))

            def norm1(b):
                dve.wait_ge(s["rstd_done"], 2 * b + 2)
                wait(dve, s["x1T_done"], b)
                for t in range(TT):
                    nc.vector.tensor_scalar(x1_tok[:, t, :], psum[:, NA, t * P:(t + 1) * P], mv[:, t, 0:1],
                                            rstd[:, t:t + 1], ALU.subtract, ALU.mult).then_inc(s["x1_done"], 1)

            def x1T_part(b):
                dve.wait_ge(s["x1T_hi_done"], b + 1)
                nc.vector.tensor_tensor(xT[:, b, 1, :], psum[:, NA, :], bits(xT[:, b, 0, :]),
                                        ALU.subtract).then_inc(s["x1T_lo_done"], 1)

            def route1(b):
                dve.wait_ge(s["logit_done"], b + 1)
                wait(dve, s["c_done"], b)
                nc.vector.tensor_copy(logit[:], psum[:, NB, :].rearrange("p (t m) -> p t m", t=TT)[:, :, 0:NE]
                                      ).then_inc(s["logit_out"], 1)
                dve.wait_ge(s["logit_out"], b + 1)
                nc.vector.tensor_reduce(top[:], logit[:], AX.X, ALU.max).then_inc(s["route_step"], 1)
                dve.wait_ge(s["route_step"], ROUTE * b + 1)
                nc.vector.tensor_tensor(shifted[:], logit[:], over_experts(top), ALU.subtract).then_inc(s["shifted"], 1)
                other, own = logit[:].unsqueeze(2), logit[:].unsqueeze(3)
                shape = [P, TT, NE, NE]
                nc.vector.tensor_tensor(above[:], other.broadcast_to(shape), own.broadcast_to(shape),
                                        ALU.is_gt).then_inc(s["route_step"], 1)
                nc.vector.tensor_tensor(tied[:], other.broadcast_to(shape), own.broadcast_to(shape),
                                        ALU.is_equal).then_inc(s["route_step"], 1)
                dve.wait_ge(s["route_step"], ROUTE * b + 3)
                nc.vector.tensor_tensor(tied[:], tied[:], before[:].unsqueeze(1).broadcast_to(shape),
                                        ALU.mult).then_inc(s["route_step"], 1)
                dve.wait_ge(s["route_step"], ROUTE * b + 4)
                nc.vector.tensor_tensor(above[:], above[:], tied[:], ALU.add).then_inc(s["route_step"], 1)
                dve.wait_ge(s["route_step"], ROUTE * b + 5)
                nc.vector.tensor_reduce(chosen[:], above[:], AX.X, ALU.add).then_inc(s["route_step"], 1)

            def route2(b):
                dve.wait_ge(s["route_step"], ROUTE * b + 6)
                dve.wait_ge(s["exp_logit"], b + 1)
                nc.vector.scalar_tensor_tensor(weight[:], chosen[:], 2.0, expl[:], ALU.is_lt,
                                               ALU.mult).then_inc(s["route_step"], 1)
                dve.wait_ge(s["route_step"], ROUTE * b + 7)
                nc.vector.tensor_reduce(wsum[:], weight[:], AX.X, ALU.add).then_inc(s["route_step"], 1)
                dve.wait_ge(s["route_step"], ROUTE * b + 8)
                nc.vector.reciprocal(rwsum[:], wsum[:]).then_inc(s["route_step"], 1)
                dve.wait_ge(s["route_step"], ROUTE * b + 9)
                wait(dve, s["cT_done"], b)
                nc.vector.tensor_tensor(combine[:], weight[:], over_experts(rwsum), ALU.mult).then_inc(s["c_done"], 1)

            ROUTE = 9

            def over_experts(v):
                return v[:].unsqueeze(2).broadcast_to([P, TT, NE])

            def cT_part(b, j):
                dve.wait_ge(s["cT_hi_done"], b + 1)
                nc.vector.tensor_tensor(cT[CLO:CLO + NE, j, :], psum[0:NE, NA, :], bits(cT[0:NE, j, :]),
                                        ALU.subtract).then_inc(s["cT_lo_done"], 1)

            def gate_part(k, e):
                dve.wait_ge(s["silu_done"], k + 1)
                dve.wait_ge(s["cb_done"], k + 1)
                wait(dve, s["g_lo_done"], k - 1)
                nc.vector.tensor_tensor(gated[e % 2], silu[e % 2],
                                        psum[:, CB, :].unsqueeze(1).broadcast_to([P, FC, S]),
                                        ALU.mult).then_inc(s["gated"], 1)

            def sum_part(b):
                dve.wait_ge(s["y_done"], NE * (b + 1))
                wait(dve, s["sum_tok_done"], b)
                nc.vector.tensor_tensor(sumT, psum[:, Y, :], bits(xT[:, b, 0, :]), ALU.add).then_inc(s["sum_half"], 1)
                dve.wait_ge(s["sum_half"], b + 1)
                nc.vector.tensor_tensor(sumT, sumT, bits(xT[:, b, 1, :]), ALU.add).then_inc(s["sum_done"], 1)

            def stats2_part(b):
                norm_stats(NB, stats2, mv2, b, "sum_tok_done", "stats2_done", "mv2_done", ("norm2_done", TT))

            def norm2(b):
                dve.wait_ge(s["rstd2_done"], 2 * b + 2)
                wait(dve, s["x_out"], DMA * b)
                for t in range(TT):
                    nc.vector.tensor_scalar(out_tok[:, t, :], psum[:, NB, t * P:(t + 1) * P], mv2[:, t, 0:1],
                                            rstd2[:, t:t + 1], ALU.subtract, ALU.mult).then_inc(s["norm2_done"], 1)

            stats1(0)
            norm1(0)
            x1T_part(0)
            route1(0)
            route2(0)
            dve.wait_ge(s["xt_cleared"], 1)
            cT_part(0, 0)
            gate_part(0, 0)

            def chunk(b, j):
                nxt = not last_step(b, NE)
                for e in range(NE):
                    k = b * NE + e
                    if e == 0 and not is_first(b):
                        sum_part(b - 1)
                    if not last_step(b, e + 1):
                        gate_part(k + 1, (e + 1) % NE)
                    if e == 0 and nxt:
                        stats1(b + 1)
                    if e == 1:
                        if nxt:
                            norm1(b + 1)
                        if not is_first(b):
                            stats2_part(b - 1)
                    if e == 2:
                        if not is_first(b):
                            norm2(b - 1)
                        if nxt:
                            x1T_part(b + 1)
                    if nxt:
                        if e == 4:
                            route1(b + 1)
                        if e == 5:
                            route2(b + 1)
                            cT_part(b + 1, 1 - j)

            chunks(dve, chunk)
            sum_part(B - 1)
            stats2_part(B - 1)
            norm2(B - 1)


_INS = ["L0_attn_x", "L0_attn_w_q", "L0_attn_w_k", "L0_attn_w_v", "L0_attn_w_o", "L0_ffn_gate_w", "L0_ffn_w1",
        "L0_ffn_w2"]


def kernel(**inputs):
    import numpy as np
    import concourse.bacc as bacc
    from concourse import mybir as mb
    from concourse.bass_utils import run_bass_kernel_spmd

    nc = bacc.Bacc("TRN2", target_bir_lowering=False, num_devices=1)
    arrays, args = {}, []
    for name in _INS:
        a = np.ascontiguousarray(inputs[name])
        arrays[f"{name}_dram"] = a
        args.append(nc.dram_tensor(f"{name}_dram", a.shape, mb.dt.from_np(a.dtype), kind="ExternalInput").ap())
    shape = inputs["L0_attn_x"].shape
    args.append(nc.dram_tensor("out_dram", shape, F32, kind="ExternalOutput").ap())
    attention_moe_kernel(nc, *args)
    r = run_bass_kernel_spmd(nc, [arrays], core_ids=[0])
    return r.results[0]["out_dram"]
```

```python
from contextlib import ExitStack

import concourse.bass as bass
from concourse import mybir

F32 = mybir.dt.float32
F32R = mybir.dt.float32r
ALU = mybir.AluOpType
ACT = mybir.ActivationFunctionType
AX = mybir.AxisListType

P = 128


def attention_moe_kernel(nc, x, w_q, w_k, w_v, w_o, gate_w, w1, w2, out):
    B, S, D = x.shape
    H, _, DK = w_q.shape
    NE, _, F = w1.shape
    HP = H // 2
    PAIRS = B * HP
    TT = S // P
    NT = B * TT
    FC = F // P
    EXT = DK + 1
    SCALE = 1.0 / DK ** 0.5
    EPS = 1e-5
    STEPS = NE * B
    DMA = 16
    STACK = 2 * DMA
    assert D == P and 2 * DK == P and S == 512 and HP == B and F == 2 * P

    with ExitStack() as ctx:
        def sb(name, shape, dt=F32):
            return ctx.enter_context(nc.sbuf_tensor(name, shape, dt))

        def sem(name):
            return ctx.enter_context(nc.semaphore(name))

        x_tok = sb("x_tok", [P, NT, D])
        acc = sb("acc", [P, B, S])
        xT = sb("xT", [P, B, 2, S], F32R)
        w_tab = sb("w_tab", [P, HP, 4, 2, P], F32R)
        ident = sb("ident", [P, P])
        w1_tab = sb("w1_tab", [P, NE, 2, F], F32R)
        w2_tab = sb("w2_tab", [P, NE, FC, 2, D], F32R)
        gate_raw = sb("gate_raw", [P, NE])
        ones = sb("ones", [P, DK])
        probs_even = sb("probs_even", [P, 2, TT, S])
        probs = [probs_even[:], x_tok[:].rearrange("p t d -> p (t d)").rearrange("p (h t s) -> p h t s", h=2, t=TT)]
        w_raw = acc[:].rearrange("p b s -> p (b s)").rearrange("p (w n) -> p w n", w=4)
        w1_raw = probs_even[:, 0].rearrange("p t s -> p (t s)").rearrange("p (e f) -> p e f", e=NE)
        w2_raw = probs_even[:, 1].rearrange("p t s -> p (t s)").rearrange("p (e c d) -> p e c d", e=NE, c=FC)
        wqk_cur = [sb(f"wqk_cur{j}", [P, 2, 2, P], F32R) for j in range(2)]
        wo_cur = sb("wo_cur", [P, 2, P], F32R)
        xT_cur = sb("xT_cur", [P, 2, S], F32R)
        q_pair, k_pair = (sb(n, [P, 2, S], F32R) for n in ("q_pair", "k_pair"))
        q_stack = [sb(f"q_stack{j}", [P, 2, 2, S], F32R) for j in range(2)]
        k_stack = [sb(f"k_stack{j}", [P, 2, 2, S], F32R) for j in range(2)]
        MAX_ROW = 96
        max_row = [[q_stack[j][MAX_ROW:MAX_ROW + TT, h, 1, 0:P] for h in range(2)] for j in range(2)]
        neg_max = [sb(f"neg_max{h}", [P, TT], F32R) for h in range(2)]
        v = sb("v", [P, 2, TT, 2, DK])
        probs_sum = [sb(f"probs_sum{h}", [P, S]) for h in range(2)]
        zT = sb("zT", [P, S])
        zT_hi, zT_lo = (sb(n, [P, S], F32R) for n in ("zT_hi", "zT_lo"))

        psum = ctx.enter_context(nc.psum_tensor("psum", [P, 8, 512], F32))
        COARSE, MISC, Z = 4, 6, 7

        g_hi = [stack[j][:, 0] for stack in (q_stack, k_stack) for j in range(2)]
        g_lo = [stack[j][:, 1] for stack in (q_stack, k_stack) for j in range(2)]
        GB = len(g_hi)
        silu = [probs_even[:, 0, FC * j:FC * (j + 1), :] for j in range(2)]
        gated = [probs_even[:, 1, FC * j:FC * (j + 1), :] for j in range(2)]
        gate_tab = wqk_cur[0][:, 0]
        cT = xT_cur
        CLO = 32
        select_e = k_pair[:].rearrange("p a s -> p (a s)").rearrange("p (e m) -> p e m", e=NE)
        x1_tok = zT[:].rearrange("p (t d) -> p t d", t=TT)
        logitT, sumT = (v[:, j].rearrange("p t h v -> p (t h v)") for j in range(2))
        x_flat, carved = x_tok[:].rearrange("p t d -> p (t d)"), [0]

        def carve(*shape):
            n = 1
            for d in shape:
                n *= d
            ap = x_flat[:, carved[0]:carved[0] + n]
            carved[0] += n
            names = " ".join("abc"[:len(shape)])
            return ap.rearrange(f"p ({names}) -> p {names}", **dict(zip("abc", shape))) if len(shape) > 1 else ap

        select_raw = carve(NE, P)
        exponent = carve(TT)
        before = carve(NE, NE)
        accT_cur = carve(S)
        out_tok = carve(TT, D)
        stats, stats2 = carve(TT, 6), carve(TT, 6)
        mv, mv2 = carve(TT, 2), carve(TT, 2)
        veps, veps2, rstd, rstd2, top, wsum, rwsum = (carve(TT) for _ in range(7))
        logit, shifted, expl, chosen, weight, combine = (carve(TT, NE) for _ in range(6))
        above, tied = carve(TT, NE, NE), carve(TT, NE, NE)
        CB, Y, NA, NB = 4, 5, 6, 7

        names = """x_in w_in ident_set ones_set zeroed w_split gate_split
            xT_done xT_hi_done xT_lo_done acc_set
            wo_cur_in xT_cur_in
            q_done k_done vT_done q_hi_done q_lo_done k_hi_done k_lo_done v_done
            coarse_done max_done maxT_done max_row_done
            scores_done exp_done added pv_done sums_done sums_out z_done r_done
            zT_hi_done zT_lo_done wo_done acc_done
            experts_in x_out xt_cleared gate_in gate_set experts_hi experts_split sel_set const_set
            accT_in tok_done mv_done rstd_done x1_done x1T_done x1T_hi_done x1T_lo_done
            logitT_done logitT_out logit_done logit_out shifted route_step exp_logit c_done cT_done cT_hi_done cT_lo_done
            h_done cb_done silu_done gated g_hi_done g_lo_done y_done
            sum_half sum_done sum_tok_done mv2_done rstd2_done stats_done stats2_done norm2_done""".split()
        s = {n: sem(n) for n in names}
        q_stacked, k_stacked = ([[sem(f"{n}_stacked{j}{h}") for h in range(2)] for j in range(2)] for n in "qk")
        wqk_cur_in = [sem(f"wqk_cur_in{j}") for j in range(2)]
        shift_in = [sem(f"shift_in{h}") for h in range(2)]
        w_sem = [sem(f"w_in{k}") for k in range(4)]

        def wait(eng, semaphore, value):
            if not isinstance(value, int) or value > 0:
                eng.wait_ge(semaphore, value)

        def wait_apart(eng, *pairs):
            pairs = [(semaphore, v if isinstance(v, int) else eng.to_reg(v)) for semaphore, v in pairs]
            if not all(isinstance(v, int) for _, v in pairs):
                eng.wait_ge(s["ident_set"], 1)
            for semaphore, v in pairs:
                wait(eng, semaphore, v)

        def bits(ap):
            return ap.bitcast(F32)

        def loops(eng, body):
            for n in range(4):
                body(n, n % 2)
            with eng.Fori(2, PAIRS // 2 - 1) as i:
                body(i * 2, 0)
                body(i * 2 + 1, 1)
            body(PAIRS - 2, 0)
            body(PAIRS - 1, 1)

        def chunks(eng, body):
            body(0, 0)
            body(1, 1)
            with eng.Fori(1, B // 2 - 1) as i:
                body(i * 2, 0)
                body(i * 2 + 1, 1)
            body(B - 2, 0)
            body(B - 1, 1)

        def is_first(n):
            return isinstance(n, int) and n == 0

        def past(b, ahead):
            return isinstance(b, int) and b + ahead >= B

        def last_step(b, ahead):
            return isinstance(b, int) and b == B - 1 and ahead >= NE

        def is_last(n, ahead):
            return isinstance(n, int) and n + ahead >= PAIRS

        x_dram = x.rearrange("b (t p) d -> p (b t) d", p=P)
        w1_dram = w1.rearrange("e d f -> d e f")
        w2_dram = w2.rearrange("e (c p) d -> p e c d", p=P)
        w_dram = [w.rearrange("h d k -> d h k") for w in (w_q, w_k, w_v)]
        out_dram = out.rearrange("b (t p) d -> p (b t) d", p=P)

        block = ctx.enter_context(nc.Block())

        @block.sync
        def _(sp):
            for k in range(3):
                sp.dma_start(w_raw[:, k, :].rearrange("p (h k) -> p h k", h=H), w_dram[k]).then_inc(w_sem[k], DMA)
            sp.dma_start(gate_raw[:], gate_w).then_inc(s["gate_in"], DMA)
            for b in range(B):
                sp.dma_start(x_tok[:, b * TT:(b + 1) * TT, :], x_dram[:, b * TT:(b + 1) * TT, :]).then_inc(s["x_in"], DMA)
                if b == 0:
                    sp.dma_start(w_raw[:, 3, :].rearrange("p (c d) -> p c d", c=HP),
                                 w_o.rearrange("(c p) d -> p c d", p=P)).then_inc(w_sem[3], DMA)

            def load_wqk(m, j):
                wait_apart(sp, (s["k_done"], m - 1))
                sp.dma_start(bits(wqk_cur[j][:]), bits(w_tab[:, m % HP, 0:2])).then_inc(wqk_cur_in[j], DMA)

            def load_xT(m):
                wait_apart(sp, (s["vT_done"], m // 2))
                sp.dma_start(bits(xT_cur[:]), bits(xT[:, m // HP])).then_inc(s["xT_cur_in"], DMA)

            def stack_q(j, m, h):
                wait_apart(sp, (s["scores_done"], 4 * (m - 2) + 2 * h + 2), (s["q_hi_done"], m + 1), (s["q_lo_done"], m + 1))
                half = slice(h * DK, (h + 1) * DK)
                sp.dma_start(bits(q_stack[j][0:DK, h]), bits(q_pair[half])).then_inc(q_stacked[j][h], DMA)
                sp.dma_start(bits(q_stack[j][DK:P, h, 0]), bits(q_pair[half, 0])).then_inc(q_stacked[j][h], DMA)

            def stack_k(j, m, h):
                wait_apart(sp, (s["scores_done"], 4 * (m - 2) + 2 * h + 2), (s["k_hi_done"], m + 1), (s["k_lo_done"], m + 1))
                half = slice(h * DK, (h + 1) * DK)
                sp.dma_start(bits(k_stack[j][0:DK, h]),
                             bits(k_pair[half, 0:1]).broadcast_to([DK, 2, S])).then_inc(k_stacked[j][h], DMA)
                sp.dma_start(bits(k_stack[j][DK:P, h, 0]), bits(k_pair[half, 1])).then_inc(k_stacked[j][h], DMA)

            def load_shift(j, h, k):
                wait(sp, s["max_row_done"], k + 1)
                sp.dma_start(bits(q_stack[j][DK:EXT, h, 1, :]), bits(max_row[j][h])).then_inc(shift_in[h], DMA)

            sp.dma_start(w1_raw, w1_dram).then_inc(s["experts_in"], DMA)
            sp.dma_start(w2_raw, w2_dram).then_inc(s["experts_in"], DMA)
            sp.wait_ge(s["w_split"], 4)
            sp.wait_ge(s["xT_hi_done"], 1)
            sp.wait_ge(s["xT_lo_done"], 1)
            load_wqk(0, 0)
            load_wqk(1, 1)
            load_wqk(2, 0)
            for m in range(2):
                for h in range(2):
                    stack_q(m, m, h)
                    stack_k(m, m, h)
            load_shift(0, 0, 0)
            sp.wait_ge(s["xT_hi_done"], B)
            sp.wait_ge(s["xT_lo_done"], B)

            def load_wo(m):
                wait_apart(sp, (s["wo_done"], m))
                sp.dma_start(bits(wo_cur[:]), bits(w_tab[:, m % HP, 3])).then_inc(s["wo_cur_in"], DMA)

            def body(n, j):
                if j == 0:
                    load_xT(n)
                load_shift(j, 1, 2 * n + 1)
                if not is_last(n, 2):
                    stack_q(j, n + 2, 0)
                if not is_last(n, 3):
                    load_wqk(n + 3, 1 - j)
                if not is_last(n, 1):
                    load_shift(1 - j, 0, 2 * n + 2)
                if not is_last(n, 2):
                    stack_q(j, n + 2, 1)
                    stack_k(j, n + 2, 0)
                if not is_first(n):
                    load_wo(n - 1)
                if not is_last(n, 2):
                    stack_k(j, n + 2, 1)

            loops(sp, body)
            load_wo(PAIRS - 1)

            def load_accT(b):
                wait_apart(sp, (s["tok_done"], b))
                sp.dma_start(accT_cur[:], acc[:, b, :]).then_inc(s["accT_in"], DMA)

            def store(b):
                wait_apart(sp, (s["norm2_done"], TT * (b + 1)))
                sp.dma_start(out_dram[:, bass.ds(b * TT, TT), :], out_tok).then_inc(s["x_out"], DMA)

            sp.wait_ge(s["acc_done"], PAIRS)
            load_accT(0)
            load_accT(1)

            def chunk(b, j):
                if not past(b, 2):
                    load_accT(b + 2)
                if not is_first(b):
                    store(b - 1)

            chunks(sp, chunk)
            store(B - 1)
            sp.wait_ge(s["x_out"], DMA * B)

        @block.gpsimd
        def _(pool):
            nc.gpsimd.memset(ident[:], 0.0).then_inc(s["zeroed"], 1)
            pool.wait_ge(s["zeroed"], 1)
            nc.gpsimd.affine_select(out=ident[:], in_=ident[:], compare_op=ALU.not_equal, fill=1.0, base=0,
                                    pattern=[[-1, P]], channel_multiplier=1).then_inc(s["ident_set"], 1)
            pool.wait_ge(s["ident_set"], 1)
            nc.gpsimd.memset(ones[:], 1.0).then_inc(s["ones_set"], 1)
            for j in range(2):
                pool.wait_ge(s["ones_set"], j + 1)
                nc.gpsimd.memset(bits(k_stack[j][DK:EXT, :, 1, :]), 1.0).then_inc(s["ones_set"], 1)
            pool.wait_ge(s["ones_set"], 3)

            def add_probs(n, j, h):
                wait(pool, s["sums_done"], n)
                for c in range(1, TT):
                    pool.wait_ge(s["exp_done"], 4 * n + 2 * h + (1 if c == 1 else 2))
                    if c > 1:
                        pool.wait_ge(s["added"], (TT - 1) * (2 * n + h) + c - 1)
                    left = probs[j][:, h, 0, :] if c == 1 else probs_sum[h][:]
                    nc.gpsimd.tensor_tensor(probs_sum[h][:], left, probs[j][:, h, c, :], ALU.add).then_inc(s["added"], 1)

            def body(n, j):
                if not is_first(n):
                    add_probs(n - 1, 1 - j, 1)
                add_probs(n, j, 0)

            def split_experts():
                pool.wait_ge(s["experts_in"], 2 * DMA)
                tables = [(w1_tab, w1_raw), (w2_tab, w2_raw)]
                n = 0
                for tab, raw in tables:
                    for e in range(NE):
                        part = (lambda q: tab[:, e, q]) if tab is w1_tab else (lambda q: tab[:, e, :, q])
                        nc.gpsimd.tensor_scalar(part(0), raw[:, e], 1.0, 0.0, ALU.mult, ALU.add).then_inc(s["experts_hi"], 1)
                        n += 1
                        pool.wait_ge(s["experts_hi"], n)
                        nc.gpsimd.tensor_tensor(part(1), raw[:, e], bits(part(0)), ALU.subtract).then_inc(s["experts_split"], 1)

            split_experts()
            loops(pool, body)
            add_probs(PAIRS - 1, 1, 1)
            pool.wait_ge(s["k_done"], PAIRS)
            nc.gpsimd.memset(bits(gate_tab), 0.0).then_inc(s["gate_set"], 1)

            def rstd_part(sem_in, sem_out, mvs, v, r, b):
                wait_apart(pool, (s[sem_in], TT * (b + 1)))
                nc.gpsimd.tensor_scalar(v[:], mvs[:, :, 1], 1.0, EPS, ALU.mult, ALU.add).then_inc(s[sem_out], 1)
                pool.wait_ge(s[sem_out], 2 * b + 1)
                nc.gpsimd.tensor_tensor(r[:], v[:], exponent, ALU.pow).then_inc(s[sem_out], 1)

            def g_lo_part(k, e):
                pool.wait_ge(s["g_hi_done"], k + 1)
                nc.gpsimd.tensor_tensor(g_lo[e % GB], gated[e % 2], bits(g_hi[e % GB]), ALU.subtract).then_inc(s["g_lo_done"], 1)

            pool.wait_ge(s["pv_done"], PAIRS)
            nc.gpsimd.memset(exponent, -0.5).then_inc(s["const_set"], 1)
            nc.gpsimd.memset(before, 0.0).then_inc(s["const_set"], 1)
            pool.wait_ge(s["const_set"], 2)
            nc.gpsimd.affine_select(out=before, in_=before, compare_op=ALU.is_ge, fill=1.0, base=0,
                                    pattern=[[-1, NE], [1, NE]], channel_multiplier=0).then_inc(s["const_set"], 1)
            nc.gpsimd.memset(select_raw, 0.0).then_inc(s["sel_set"], 1)
            pool.wait_ge(s["sel_set"], 1)
            for i, first in enumerate((0, CLO)):
                nc.gpsimd.affine_select(out=select_raw, in_=select_raw, compare_op=ALU.not_equal, fill=1.0,
                                        base=-first, pattern=[[-1, NE], [0, P]], channel_multiplier=1).then_inc(s["sel_set"], 1)
                pool.wait_ge(s["sel_set"], i + 2)
            pool.wait_ge(s["scores_done"], 4 * PAIRS)
            nc.gpsimd.tensor_scalar(select_e, select_raw, 1.0, 0.0, ALU.mult, ALU.add).then_inc(s["sel_set"], 1)
            nc.gpsimd.memset(bits(cT[:]), 0.0).then_inc(s["xt_cleared"], 1)
            rstd_part("mv_done", "rstd_done", mv, veps, rstd, 0)
            g_lo_part(0, 0)
            rstd_part("mv_done", "rstd_done", mv, veps, rstd, 1)
            g_lo_part(1, 1)

            def chunk(b, j):
                for e in range(NE):
                    if not last_step(b, e + 2):
                        g_lo_part(b * NE + e + 2, (e + 2) % NE)
                    if e == 3 and not is_first(b):
                        rstd_part("mv2_done", "rstd2_done", mv2, veps2, rstd2, b - 1)
                    if e == 5 and not past(b, 2):
                        rstd_part("mv_done", "rstd_done", mv, veps, rstd, b + 2)

            chunks(pool, chunk)
            rstd_part("mv2_done", "rstd2_done", mv2, veps2, rstd2, B - 1)

        @block.tensor
        def _(pe):
            pe.wait_ge(s["ident_set"], 1)
            pe.wait_ge(s["x_in"], DMA * B)
            for b in range(B):
                wait(pe, s["xT_hi_done"], b - 3)
                wait(pe, s["xT_lo_done"], b - 3)
                wait(pe, s["acc_set"], b - 3)
                for t in range(TT):
                    mm = nc.tensor.transpose(psum[:, b % 4, t * P:(t + 1) * P], x_tok[:, b * TT + t, :], ident[:])
                mm.then_inc(s["xT_done"], 1)

            def product(dst, left, right, start=True, stop=True):
                (lh, ll), (rh, rl) = left, right
                nc.tensor.matmul(dst, lh, rh, start=start, stop=False)
                nc.tensor.matmul(dst, lh, rl, start=False, stop=False)
                return nc.tensor.matmul(dst, ll, rh, start=False, stop=stop)

            def project_qk(which, m, j):
                w = [wqk_cur[j][:, which, part, :] for part in range(2)]
                return product(psum[:, MISC, :], w, [xT[:, m // HP, part, :] for part in range(2)])

            def project_q(m, i, j):
                pe.wait_ge(wqk_cur_in[j], DMA * (i + 1))
                wait(pe, s["k_hi_done"], m)
                wait(pe, s["k_lo_done"], m)
                project_qk(0, m, j).then_inc(s["q_done"], 1)

            def project_k(m, j):
                pe.wait_ge(s["q_hi_done"], m + 1)
                pe.wait_ge(s["q_lo_done"], m + 1)
                wait(pe, s["sums_out"], m - 2)
                project_qk(1, m, j).then_inc(s["k_done"], 1)

            def project_v(m):
                pe.wait_ge(s["xT_cur_in"], DMA * (m // 2 + 1))
                pe.wait_ge(s["exp_done"], 4 * m + 4)
                for t in range(TT):
                    tok = slice(t * P, (t + 1) * P)
                    mm = product(psum[:, 2 + t // 2, t % 2 * 2 * P:(t % 2 + 1) * 2 * P], [xT_cur[:, part, tok] for part in range(2)],
                                 [w_tab[:, bass.ds(m % HP, 2), 2, part, :] for part in range(2)])
                mm.then_inc(s["vT_done"], 1)

            def coarse(n, i, j, h, t):
                k = 2 * n + h
                if t == 0:
                    pe.wait_ge(q_stacked[j][h], STACK * (i + 1))
                    pe.wait_ge(k_stacked[j][h], STACK * (i + 1))
                wait(pe, s["max_done"], TT * k + t - 1)
                if t == 1:
                    wait(pe, s["max_row_done"], k)
                nc.tensor.matmul(psum[:, COARSE + t % 2, :], q_stack[j][:, h, 0, t * P:(t + 1) * P], k_stack[j][:, h, 0, :],
                                 start=True, stop=True).then_inc(s["coarse_done"], 1)

            def shift_rows(n, h):
                k = 2 * n + h
                pe.wait_ge(s["max_done"], TT * (k + 1))
                nc.tensor.transpose(psum[0:TT, COARSE + 1, 0:P], bits(neg_max[h][:]), ident[:]).then_inc(s["maxT_done"], 1)

            def scores(n, j, h, groups=range(2)):
                k = 2 * n + h
                if groups[0] == 0:
                    pe.wait_ge(shift_in[h], DMA * (n + 1))
                for g in groups:
                    wait(pe, s["exp_done"], 2 * (k - 1) + g + 1)
                    if j == 1 and h == 0 and g == 1:
                        pe.wait_ge(s["v_done"], (n - 1) // 2 + 1)
                    for t in range(2 * g, 2 * g + 2):
                        keys = slice(t * P, (t + 1) * P)
                        nc.tensor.matmul(psum[:, t, :], k_stack[j][:, h, 0, keys], q_stack[j][:, h, 0, :], start=True, stop=False)
                        mm = nc.tensor.matmul(psum[:, t, :], k_stack[j][0:EXT, h, 1, keys], q_stack[j][0:EXT, h, 1, :], start=False, stop=True)
                    mm.then_inc(s["scores_done"], 1)

            def times_v(n, j, c):
                if c == 0:
                    pe.wait_ge(s["exp_done"], 4 * n + 4)
                    pe.wait_ge(s["v_done"], (n - j) // 2 + 1)
                    wait(pe, s["z_done"], n)
                for h in range(2):
                    mm = nc.tensor.matmul(psum[h * DK:(h + 1) * DK, Z, :], v[:, j, c, h, :], probs[j][:, h, c, :],
                                          start=(c == 0), stop=(c == TT - 1))
                if c == TT - 1:
                    mm.then_inc(s["pv_done"], 1)

            def sum_probs(n, j):
                pe.wait_ge(s["added"], (TT - 1) * 2 * (n + 1))
                pe.wait_ge(s["q_hi_done"], n + 4 if not is_last(n, 3) else PAIRS)
                pe.wait_ge(s["q_lo_done"], n + 4 if not is_last(n, 3) else PAIRS)
                if is_last(n, 1):
                    pe.wait_ge(s["acc_done"], n - 1)
                for h in range(2):
                    mm = nc.tensor.matmul(psum[h * DK:(h + 1) * DK, MISC, :], ones[:], probs_sum[h][:], start=True, stop=True)
                mm.then_inc(s["sums_done"], 1)

            def project_out(n):
                pe.wait_ge(s["zT_hi_done"], n + 1)
                pe.wait_ge(s["zT_lo_done"], n + 1)
                pe.wait_ge(s["wo_cur_in"], DMA * (n + 1))
                pe.wait_ge(s["k_hi_done"], n + 5 if not is_last(n, 4) else PAIRS)
                pe.wait_ge(s["k_lo_done"], n + 5 if not is_last(n, 4) else PAIRS)
                pe.wait_ge(s["sums_out"], n + 2 if not is_last(n, 1) else PAIRS)
                if is_last(n, 1):
                    pe.wait_ge(s["acc_done"], n)
                mm = product(psum[:, MISC, :], [wo_cur[:, 0, :], wo_cur[:, 1, :]], [zT_hi[:], zT_lo[:]])
                mm.then_inc(s["wo_done"], 1)

            for m in range(2):
                project_q(m, 0, m)
                project_k(m, m)
            pe.wait_ge(s["ones_set"], 3)
            for h in range(2):
                for t in range(TT):
                    coarse(0, 0, 0, h, t)
                if h == 0:
                    shift_rows(0, 0)

            def body(n, j):
                ahead, project = not is_last(n, 1), not is_last(n, 2)

                def turn(m, parity):
                    return (m - parity) // 2

                former, before_former = not is_first(n), not (isinstance(n, int) and n < 2)

                def next_coarse(h, t):
                    if ahead:
                        coarse(n + 1, turn(n + 1, 1 - j), 1 - j, h, t)

                scores(n, j, 0)
                shift_rows(n, 1)
                next_coarse(0, 0)
                if project:
                    project_q(n + 2, turn(n + 2, j), j)
                next_coarse(0, 1)
                if former:
                    times_v(n - 1, 1 - j, 0)
                next_coarse(0, 2)
                if former:
                    times_v(n - 1, 1 - j, 1)
                    sum_probs(n - 1, 1 - j)
                next_coarse(0, 3)
                scores(n, j, 1, (0,))
                if ahead:
                    shift_rows(n + 1, 0)
                if project:
                    project_k(n + 2, j)
                scores(n, j, 1, (1,))
                next_coarse(1, 0)
                if former:
                    times_v(n - 1, 1 - j, 2)
                if before_former:
                    project_out(n - 2)
                next_coarse(1, 1)
                if j == 0:
                    project_v(n)
                next_coarse(1, 2)
                if former:
                    times_v(n - 1, 1 - j, 3)
                next_coarse(1, 3)

            loops(pe, body)
            sum_probs(PAIRS - 1, 1)
            for c in range(TT):
                times_v(PAIRS - 1, 1, c)
            project_out(PAIRS - 2)
            project_out(PAIRS - 1)

            def to_tokens(b):
                pe.wait_ge(s["accT_in"], DMA * (b + 1))
                wait(pe, s["cT_hi_done"], b)
                wait(pe, s["cT_lo_done"], b)
                for t in range(TT):
                    mm = nc.tensor.transpose(psum[:, NA, t * P:(t + 1) * P], accT_cur[:, t * P:(t + 1) * P], ident[:])
                mm.then_inc(s["tok_done"], 1)

            def transpose_x1(b):
                pe.wait_ge(s["x1_done"], TT * (b + 1))
                for t in range(TT):
                    mm = nc.tensor.transpose(psum[:, NA, t * P:(t + 1) * P], x1_tok[:, t, :], ident[:])
                mm.then_inc(s["x1T_done"], 1)

            def route(b):
                pe.wait_ge(s["x1T_hi_done"], b + 1)
                pe.wait_ge(s["x1T_lo_done"], b + 1)
                wait(pe, s["norm2_done"], TT * (b - 2))
                product(psum[:, NB, :], [gate_tab[:, 0, :], gate_tab[:, 1, :]],
                        [xT[:, b, 0, :], xT[:, b, 1, :]]).then_inc(s["logitT_done"], 1)

            def logits_to_tokens(b):
                pe.wait_ge(s["logitT_out"], b + 1)
                for t in range(TT):
                    mm = nc.tensor.transpose(psum[:, NB, t * P:(t + 1) * P], logitT[:, t * P:(t + 1) * P], ident[:])
                mm.then_inc(s["logit_done"], 1)

            def transpose_c(b):
                pe.wait_ge(s["c_done"], b + 1)
                for t in range(TT):
                    mm = nc.tensor.transpose(psum[0:NE, NA, t * P:(t + 1) * P], combine[:, t, :], ident[:])
                mm.then_inc(s["cT_done"], 1)

            def hidden(k, b, e):
                wait(pe, s["silu_done"], k - 1)
                for f in range(FC):
                    cols = slice(f * P, (f + 1) * P)
                    mm = product(psum[:, FC * (e % 2) + f, :], [w1_tab[:, e, 0, cols], w1_tab[:, e, 1, cols]],
                                 [xT[:, b, 0, :], xT[:, b, 1, :]])
                mm.then_inc(s["h_done"], 1)

            def spread_c(k, b, j, e):
                if e == 0:
                    pe.wait_ge(s["cT_hi_done"], b + 1)
                    pe.wait_ge(s["cT_lo_done"], b + 1)
                wait(pe, s["gated"], k)
                nc.tensor.matmul(psum[:, CB, :], select_e[:, e, :], cT[:, j, :], start=True,
                                 stop=True).then_inc(s["cb_done"], 1)

            def second(k, b, e):
                if e == 0:
                    wait(pe, s["sum_half"], b)
                pe.wait_ge(s["g_hi_done"], k + 1)
                for f in range(FC):
                    for part in range(2):
                        nc.tensor.matmul(psum[:, Y, :], w2_tab[:, e, f, part, :], g_hi[e % GB][:, f, :],
                                         start=(e == 0 and f == 0 and part == 0), stop=False)
                pe.wait_ge(s["g_lo_done"], k + 1)
                for f in range(FC):
                    mm = nc.tensor.matmul(psum[:, Y, :], w2_tab[:, e, f, 0, :], g_lo[e % GB][:, f, :],
                                          start=False, stop=(e == NE - 1 and f == FC - 1))
                mm.then_inc(s["y_done"], 1)

            def sum_to_tokens(b):
                pe.wait_ge(s["sum_done"], b + 1)
                wait(pe, s["logit_out"], b + 3 if not past(b, 2) else B)
                for t in range(TT):
                    mm = nc.tensor.transpose(psum[:, NB, t * P:(t + 1) * P], sumT[:, t * P:(t + 1) * P], ident[:])
                mm.then_inc(s["sum_tok_done"], 1)

            pe.wait_ge(s["gate_set"], 3)
            pe.wait_ge(s["sel_set"], 4)
            pe.wait_ge(s["experts_split"], 2 * NE)
            pe.wait_ge(s["exp_done"], 4 * PAIRS)
            pe.wait_ge(s["acc_done"], PAIRS)
            to_tokens(0)
            transpose_x1(0)
            route(0)
            logits_to_tokens(0)
            transpose_c(0)
            for e in range(3):
                hidden(e, 0, e)
                spread_c(e, 0, 0, e)
                if e == 0:
                    to_tokens(1)
            transpose_x1(1)

            def chunk(b, j):
                for e in range(NE):
                    k = b * NE + e
                    if not last_step(b, e + 3):
                        hidden(k + 3, b + (e + 3) // NE, (e + 3) % NE)
                    second(k, b, e)
                    if not last_step(b, e + 3):
                        spread_c(k + 3, b + (e + 3) // NE, (j + (e + 3) // NE) % 2, (e + 3) % NE)
                    if not past(b, 1):
                        if e == 0:
                            route(b + 1)
                        if e == 1:
                            logits_to_tokens(b + 1)
                        if e == 3:
                            transpose_c(b + 1)
                    if e == 2 and not is_first(b):
                        sum_to_tokens(b - 1)
                    if not past(b, 2):
                        if e == 4:
                            to_tokens(b + 2)
                        if e == 7:
                            transpose_x1(b + 2)

            chunks(pe, chunk)
            sum_to_tokens(B - 1)

        @block.scalar
        def _(act):
            for k in range(4):
                act.wait_ge(w_sem[k], DMA)
                nc.scalar.activation(w_tab[:, :, k, 0, :], w_raw[:, k, :].rearrange("p (c n) -> p c n", c=HP),
                                     ACT.Copy).then_inc(s["w_in"], 1)
            for b in range(B):
                act.wait_ge(s["xT_done"], b + 1)
                nc.scalar.activation(xT[:, b, 0, :], psum[:, b % 4, :], ACT.Copy).then_inc(s["xT_hi_done"], 1)
                act.wait_ge(s["w_split"], 4)
                nc.scalar.activation(acc[:, b, :], psum[:, b % 4, :], ACT.Copy, scale=2.0).then_inc(s["acc_set"], 1)

            def q_part(n, j):
                act.wait_ge(s["q_done"], n + 1)
                free_stage(q_stacked, n, j)
                nc.scalar.activation(q_pair[:, 0, :], psum[:, MISC, :], ACT.Copy, scale=SCALE).then_inc(s["q_hi_done"], 1)

            def k_part(n, j):
                act.wait_ge(s["k_done"], n + 1)
                free_stage(k_stacked, n, j)
                nc.scalar.activation(k_pair[:, 0, :], psum[:, MISC, :], ACT.Copy).then_inc(s["k_hi_done"], 1)

            def free_stage(stacked, n, j):
                for h in range(2):
                    wait(act, stacked[1 - j][h], STACK * ((n - 1 - (1 - j)) // 2 + 1))

            def v_part(m):
                act.wait_ge(s["vT_done"], m // 2 + 1)
                wait(act, s["pv_done"], m)
                nc.scalar.activation(v[:].rearrange("p j t h k -> p t j (h k)"),
                                     psum[:, 2:4, :].rearrange("p b (t j k) -> p (b t) j k", t=2, j=2),
                                     ACT.Copy).then_inc(s["v_done"], 1)

            def exps(n, j, h, groups=range(2)):
                k = 2 * n + h
                wait(act, s["pv_done"], n - 1)
                wait(act, s["sums_done"], n - 1)
                for g in groups:
                    act.wait_ge(s["scores_done"], 2 * k + g + 1)
                    nc.scalar.activation(probs[j][:, h, 2 * g:2 * g + 2, :], psum[:, 2 * g:2 * g + 2, :],
                                         ACT.Exp).then_inc(s["exp_done"], 1)

            def sums_part(n):
                act.wait_ge(s["sums_done"], n + 1)
                wait(act, s["zT_lo_done"], n)
                nc.scalar.activation(zT[:], psum[:, MISC, :], ACT.Copy).then_inc(s["sums_out"], 1)

            def zT_part(n):
                act.wait_ge(s["z_done"], n + 1)
                wait(act, s["wo_done"], n)
                nc.scalar.activation(zT_hi[:], zT[:], ACT.Copy).then_inc(s["zT_hi_done"], 1)

            for n in range(2):
                q_part(n, n)
                k_part(n, n)
            act.wait_ge(s["experts_split"], 2 * NE)

            def body(n, j):
                exps(n, j, 0, (0,))
                if not (isinstance(n, int) and n < 2):
                    zT_part(n - 2)
                exps(n, j, 0, (1,))
                if not is_last(n, 2):
                    q_part(n + 2, j)
                if not is_first(n):
                    sums_part(n - 1)
                exps(n, j, 1, (0,))
                if not is_last(n, 2):
                    k_part(n + 2, j)
                exps(n, j, 1, (1,))
                if j == 0:
                    v_part(n)

            loops(act, body)
            zT_part(PAIRS - 2)
            sums_part(PAIRS - 1)
            zT_part(PAIRS - 1)

            def x1T_part(b):
                act.wait_ge(s["x1T_done"], b + 1)
                nc.scalar.activation(xT[:, b, 0, :], psum[:, NA, :], ACT.Copy).then_inc(s["x1T_hi_done"], 1)

            def logitT_part(b):
                act.wait_ge(s["logitT_done"], b + 1)
                wait(act, s["logit_done"], b)
                nc.scalar.activation(logitT, psum[:, NB, :], ACT.Copy).then_inc(s["logitT_out"], 1)

            def exp_part(b):
                act.wait_ge(s["shifted"], b + 1)
                nc.scalar.activation(expl[:], shifted[:], ACT.Exp).then_inc(s["exp_logit"], 1)

            def cT_part(b, j):
                act.wait_ge(s["cT_done"], b + 1)
                wait(act, s["cb_done"], NE * (b - 1))
                nc.scalar.activation(cT[0:NE, j, :], psum[0:NE, NA, :], ACT.Copy).then_inc(s["cT_hi_done"], 1)

            def silu_part(k, e):
                act.wait_ge(s["h_done"], k + 1)
                wait(act, s["gated"], k - 1)
                nc.scalar.activation(silu[e % 2], psum[:, FC * (e % 2):FC * (e % 2 + 1), :],
                                     ACT.Silu).then_inc(s["silu_done"], 1)

            def g_hi_part(k, e):
                act.wait_ge(s["gated"], k + 1)
                wait(act, s["y_done"], k - GB + 1)
                nc.scalar.activation(g_hi[e % GB], gated[e % 2], ACT.Copy).then_inc(s["g_hi_done"], 1)

            x1T_part(0)
            logitT_part(0)
            exp_part(0)
            act.wait_ge(s["xt_cleared"], 1)
            cT_part(0, 0)
            silu_part(0, 0)
            for e in range(2):
                silu_part(e + 1, e + 1)
                g_hi_part(e, e)
            x1T_part(1)

            def chunk(b, j):
                for e in range(NE):
                    k = b * NE + e
                    if not last_step(b, e + 3):
                        silu_part(k + 3, (e + 3) % NE)
                    if not last_step(b, e + 2):
                        g_hi_part(k + 2, (e + 2) % NE)
                    if not past(b, 1):
                        if e == 0:
                            logitT_part(b + 1)
                        if e == 1:
                            exp_part(b + 1)
                        if e == 3:
                            cT_part(b + 1, 1 - j)
                    if e == 7 and not past(b, 2):
                        x1T_part(b + 2)

            chunks(act, chunk)

        @block.vector
        def _(dve):
            for k in range(4):
                dve.wait_ge(s["w_in"], k + 1)
                nc.vector.tensor_tensor(w_tab[:, :, k, 1, :], w_raw[:, k, :].rearrange("p (c n) -> p c n", c=HP),
                                        bits(w_tab[:, :, k, 0, :]), ALU.subtract).then_inc(s["w_split"], 1)
            for b in range(B):
                dve.wait_ge(s["acc_set"], b + 1)
                nc.vector.tensor_tensor(xT[:, b, 1, :], psum[:, b % 4, :], bits(xT[:, b, 0, :]),
                                        ALU.subtract).then_inc(s["xT_lo_done"], 1)

            def q_part(n, j):
                dve.wait_ge(s["q_hi_done"], n + 1)
                free_stage(q_stacked, n, j)
                nc.vector.scalar_tensor_tensor(q_pair[:, 1, :], psum[:, MISC, :], SCALE, bits(q_pair[:, 0, :]), ALU.mult,
                                               ALU.subtract).then_inc(s["q_lo_done"], 1)

            def k_part(n, j):
                dve.wait_ge(s["k_hi_done"], n + 1)
                free_stage(k_stacked, n, j)
                nc.vector.tensor_tensor(k_pair[:, 1, :], psum[:, MISC, :], bits(k_pair[:, 0, :]), ALU.subtract).then_inc(s["k_lo_done"], 1)

            def free_stage(stacked, n, j):
                for h in range(2):
                    wait(dve, stacked[1 - j][h], STACK * ((n - 1 - (1 - j)) // 2 + 1))

            def maxima(n, h, tiles=range(TT)):
                k = 2 * n + h
                if tiles[0] == 0:
                    wait(dve, s["maxT_done"], k - 1)
                for t in tiles:
                    dve.wait_ge(s["coarse_done"], TT * k + t + 1)
                    nc.vector.tensor_reduce(neg_max[h][:, t:t + 1], psum[:, COARSE + t % 2, :], AX.X, ALU.max,
                                            negate=True).then_inc(s["max_done"], 1)

            def shift_part(n, j, h):
                k = 2 * n + h
                dve.wait_ge(s["maxT_done"], k + 1)
                wait(dve, shift_in[h], DMA * n)
                nc.vector.tensor_copy(max_row[j][h], psum[0:TT, COARSE + 1, 0:P]).then_inc(s["max_row_done"], 1)

            def reciprocals(n, parts):
                dve.wait_ge(s["sums_out"], n + 1)
                for t in parts:
                    cols = slice(t * P, (t + 1) * P)
                    nc.vector.reciprocal(zT[:, cols], zT[:, cols]).then_inc(s["r_done"], 1)

            def z_part(n):
                dve.wait_ge(s["pv_done"], n + 1)
                dve.wait_ge(s["r_done"], TT * (n + 1))
                nc.vector.tensor_tensor(zT[:], psum[:, Z, :], zT[:], ALU.mult).then_inc(s["z_done"], 1)

            def zT_part(n):
                dve.wait_ge(s["zT_hi_done"], n + 1)
                wait(dve, s["wo_done"], n)
                nc.vector.tensor_tensor(zT_lo[:], zT[:], bits(zT_hi[:]), ALU.subtract).then_inc(s["zT_lo_done"], 1)

            def acc_part(n):
                dve.wait_ge(s["wo_done"], n + 1)
                wait(dve, s["acc_done"], n)
                a = acc[:, n // HP, :]
                nc.vector.tensor_tensor(a, psum[:, MISC, :], a, ALU.add).then_inc(s["acc_done"], 1)

            dve.wait_ge(s["acc_set"], B)
            for n in range(2):
                q_part(n, n)
                k_part(n, n)
            maxima(0, 0)
            shift_part(0, 0, 0)
            maxima(0, 1)

            def body(n, j):
                ahead, project, former = not is_last(n, 1), not is_last(n, 2), not is_first(n)

                def next_maximum(h, t):
                    if ahead:
                        maxima(n + 1, h, (t,))

                shift_part(n, j, 1)
                next_maximum(0, 0)
                if not (isinstance(n, int) and n < 2):
                    zT_part(n - 2)
                next_maximum(0, 1)
                if project:
                    q_part(n + 2, j)
                next_maximum(0, 2)
                next_maximum(0, 3)
                if former:
                    reciprocals(n - 1, (0,))
                if ahead:
                    shift_part(n + 1, 1 - j, 0)
                if former:
                    reciprocals(n - 1, (1,))
                if project:
                    k_part(n + 2, j)
                next_maximum(1, 0)
                if former:
                    reciprocals(n - 1, (2,))
                if not (isinstance(n, int) and n < 2):
                    acc_part(n - 2)
                next_maximum(1, 1)
                next_maximum(1, 2)
                if former:
                    reciprocals(n - 1, (3,))
                next_maximum(1, 3)
                if former:
                    z_part(n - 1)

            loops(dve, body)
            zT_part(PAIRS - 2)
            reciprocals(PAIRS - 1, range(TT))
            z_part(PAIRS - 1)
            acc_part(PAIRS - 2)
            zT_part(PAIRS - 1)
            acc_part(PAIRS - 1)

            dve.wait_ge(s["gate_in"], DMA)
            dve.wait_ge(s["gate_set"], 1)
            nc.vector.tensor_copy(gate_tab[:, 0, 0:NE], gate_raw[:]).then_inc(s["gate_set"], 1)
            dve.wait_ge(s["gate_set"], 2)
            nc.vector.tensor_tensor(gate_tab[:, 1, 0:NE], gate_raw[:], bits(gate_tab[:, 0, 0:NE]),
                                    ALU.subtract).then_inc(s["gate_set"], 1)

            def norm_stats(bank, st, mvs, b, tok_sem, st_sem, mv_sem, free_sem):
                dve.wait_ge(s[tok_sem], b + 1)
                wait(dve, s[mv_sem], TT * b)
                for t in range(TT):
                    nc.vector.bn_stats(st[:, t], psum[:, bank, t * P:(t + 1) * P]).then_inc(s[st_sem], 1)
                wait_apart(dve, (s[st_sem], TT * (b + 1)), (s[free_sem[0]], free_sem[1] * b))
                for t in range(TT):
                    nc.vector.bn_aggr(mvs[:, t], st[:, t]).then_inc(s[mv_sem], 1)

            def stats1(b):
                norm_stats(NA, stats, mv, b, "tok_done", "stats_done", "mv_done", ("x1_done", TT))

            def norm1(b):
                dve.wait_ge(s["rstd_done"], 2 * b + 2)
                wait(dve, s["x1T_done"], b)
                for t in range(TT):
                    nc.vector.tensor_scalar(x1_tok[:, t, :], psum[:, NA, t * P:(t + 1) * P], mv[:, t, 0:1],
                                            rstd[:, t:t + 1], ALU.subtract, ALU.mult).then_inc(s["x1_done"], 1)

            def x1T_part(b):
                dve.wait_ge(s["x1T_hi_done"], b + 1)
                nc.vector.tensor_tensor(xT[:, b, 1, :], psum[:, NA, :], bits(xT[:, b, 0, :]),
                                        ALU.subtract).then_inc(s["x1T_lo_done"], 1)

            def route1(b):
                dve.wait_ge(s["logit_done"], b + 1)
                wait(dve, s["c_done"], b)
                nc.vector.tensor_copy(logit[:], psum[:, NB, :].rearrange("p (t m) -> p t m", t=TT)[:, :, 0:NE]
                                      ).then_inc(s["logit_out"], 1)
                dve.wait_ge(s["logit_out"], b + 1)
                nc.vector.tensor_reduce(top[:], logit[:], AX.X, ALU.max).then_inc(s["route_step"], 1)
                dve.wait_ge(s["route_step"], ROUTE * b + 1)
                nc.vector.tensor_tensor(shifted[:], logit[:], over_experts(top), ALU.subtract).then_inc(s["shifted"], 1)
                other, own = logit[:].unsqueeze(2), logit[:].unsqueeze(3)
                shape = [P, TT, NE, NE]
                nc.vector.tensor_tensor(above[:], other.broadcast_to(shape), own.broadcast_to(shape),
                                        ALU.is_gt).then_inc(s["route_step"], 1)
                nc.vector.tensor_tensor(tied[:], other.broadcast_to(shape), own.broadcast_to(shape),
                                        ALU.is_equal).then_inc(s["route_step"], 1)
                dve.wait_ge(s["route_step"], ROUTE * b + 3)
                nc.vector.tensor_tensor(tied[:], tied[:], before.unsqueeze(1).broadcast_to(shape),
                                        ALU.mult).then_inc(s["route_step"], 1)
                dve.wait_ge(s["route_step"], ROUTE * b + 4)
                nc.vector.tensor_tensor(above[:], above[:], tied[:], ALU.add).then_inc(s["route_step"], 1)
                dve.wait_ge(s["route_step"], ROUTE * b + 5)
                nc.vector.tensor_reduce(chosen[:], above[:], AX.X, ALU.add).then_inc(s["route_step"], 1)

            def route2(b):
                dve.wait_ge(s["route_step"], ROUTE * b + 6)
                dve.wait_ge(s["exp_logit"], b + 1)
                nc.vector.scalar_tensor_tensor(weight[:], chosen[:], 2.0, expl[:], ALU.is_lt,
                                               ALU.mult).then_inc(s["route_step"], 1)
                dve.wait_ge(s["route_step"], ROUTE * b + 7)
                nc.vector.tensor_reduce(wsum[:], weight[:], AX.X, ALU.add).then_inc(s["route_step"], 1)
                dve.wait_ge(s["route_step"], ROUTE * b + 8)
                nc.vector.reciprocal(rwsum[:], wsum[:]).then_inc(s["route_step"], 1)
                dve.wait_ge(s["route_step"], ROUTE * b + 9)
                wait(dve, s["cT_done"], b)
                nc.vector.tensor_tensor(combine[:], weight[:], over_experts(rwsum), ALU.mult).then_inc(s["c_done"], 1)

            ROUTE = 9

            def over_experts(v):
                return v[:].unsqueeze(2).broadcast_to([P, TT, NE])

            def cT_part(b, j):
                dve.wait_ge(s["cT_hi_done"], b + 1)
                nc.vector.tensor_tensor(cT[CLO:CLO + NE, j, :], psum[0:NE, NA, :], bits(cT[0:NE, j, :]),
                                        ALU.subtract).then_inc(s["cT_lo_done"], 1)

            def gate_part(k, e):
                dve.wait_ge(s["silu_done"], k + 1)
                dve.wait_ge(s["cb_done"], k + 1)
                wait(dve, s["g_lo_done"], k - 1)
                nc.vector.tensor_tensor(gated[e % 2], silu[e % 2],
                                        psum[:, CB, :].unsqueeze(1).broadcast_to([P, FC, S]),
                                        ALU.mult).then_inc(s["gated"], 1)

            def sum_part(b):
                dve.wait_ge(s["y_done"], NE * (b + 1))
                wait(dve, s["sum_tok_done"], b)
                nc.vector.tensor_tensor(sumT, psum[:, Y, :], bits(xT[:, b, 0, :]), ALU.add).then_inc(s["sum_half"], 1)
                dve.wait_ge(s["sum_half"], b + 1)
                nc.vector.tensor_tensor(sumT, sumT, bits(xT[:, b, 1, :]), ALU.add).then_inc(s["sum_done"], 1)

            def stats2_part(b):
                norm_stats(NB, stats2, mv2, b, "sum_tok_done", "stats2_done", "mv2_done", ("norm2_done", TT))

            def norm2(b):
                dve.wait_ge(s["rstd2_done"], 2 * b + 2)
                wait(dve, s["x_out"], DMA * b)
                for t in range(TT):
                    nc.vector.tensor_scalar(out_tok[:, t, :], psum[:, NB, t * P:(t + 1) * P], mv2[:, t, 0:1],
                                            rstd2[:, t:t + 1], ALU.subtract, ALU.mult).then_inc(s["norm2_done"], 1)

            stats1(0)
            norm1(0)
            x1T_part(0)
            route1(0)
            route2(0)
            dve.wait_ge(s["xt_cleared"], 1)
            cT_part(0, 0)
            gate_part(0, 0)
            stats1(1)
            gate_part(1, 1)
            norm1(1)
            gate_part(2, 2)
            x1T_part(1)

            def chunk(b, j):
                for e in range(NE):
                    if e == 0 and not is_first(b):
                        sum_part(b - 1)
                    if not last_step(b, e + 3):
                        gate_part(b * NE + e + 3, (e + 3) % NE)
                    if not past(b, 1):
                        if e == 1:
                            route1(b + 1)
                        if e == 2:
                            route2(b + 1)
                        if e == 3:
                            cT_part(b + 1, 1 - j)
                    if not is_first(b):
                        if e == 2:
                            stats2_part(b - 1)
                        if e == 4:
                            norm2(b - 1)
                    if not past(b, 2):
                        if e == 4:
                            stats1(b + 2)
                        if e == 6:
                            norm1(b + 2)
                        if e == 7:
                            x1T_part(b + 2)

            chunks(dve, chunk)
            sum_part(B - 1)
            stats2_part(B - 1)
            norm2(B - 1)


_INS = ["L0_attn_x", "L0_attn_w_q", "L0_attn_w_k", "L0_attn_w_v", "L0_attn_w_o", "L0_ffn_gate_w", "L0_ffn_w1",
        "L0_ffn_w2"]


def kernel(**inputs):
    import numpy as np
    import concourse.bacc as bacc
    from concourse import mybir as mb
    from concourse.bass_utils import run_bass_kernel_spmd

    nc = bacc.Bacc("TRN2", target_bir_lowering=False, num_devices=1)
    arrays, args = {}, []
    for name in _INS:
        a = np.ascontiguousarray(inputs[name])
        arrays[f"{name}_dram"] = a
        args.append(nc.dram_tensor(f"{name}_dram", a.shape, mb.dt.from_np(a.dtype), kind="ExternalInput").ap())
    shape = inputs["L0_attn_x"].shape
    args.append(nc.dram_tensor("out_dram", shape, F32, kind="ExternalOutput").ap())
    attention_moe_kernel(nc, *args)
    r = run_bass_kernel_spmd(nc, [arrays], core_ids=[0])
    return r.results[0]["out_dram"]
```

```python
from contextlib import ExitStack

import concourse.bass as bass
from concourse import mybir

F32 = mybir.dt.float32
F32R = mybir.dt.float32r
ALU = mybir.AluOpType
ACT = mybir.ActivationFunctionType
AX = mybir.AxisListType

P = 128


def attention_moe_kernel(nc, x, w_q, w_k, w_v, w_o, gate_w, w1, w2, out):
    B, S, D = x.shape
    H, _, DK = w_q.shape
    NE, _, F = w1.shape
    HP = H // 2
    PAIRS = B * HP
    TT = S // P
    NT = B * TT
    FC = F // P
    EXT = DK + 1
    SCALE = 1.0 / DK ** 0.5
    EPS = 1e-5
    PEELED = 8
    SPLIT_AT = (1, 2, 4, 5)
    DMA = 16
    STACK = 2 * DMA
    assert D == P and 2 * DK == P and S == 512 and HP == B and F == 2 * P

    with ExitStack() as ctx:
        def sb(name, shape, dt=F32):
            return ctx.enter_context(nc.sbuf_tensor(name, shape, dt))

        def sem(name):
            return ctx.enter_context(nc.semaphore(name))

        x_tok = sb("x_tok", [P, NT, D])
        acc = sb("acc", [P, B, S])
        xT = sb("xT", [P, B, 2, S], F32R)
        w_tab = sb("w_tab", [P, HP, 4, 2, P], F32R)
        ident = sb("ident", [P, P])
        w1_tab = sb("w1_tab", [P, NE, 2, F], F32R)
        w2_tab = sb("w2_tab", [P, NE, FC, 2, D], F32R)
        gate_raw = sb("gate_raw", [P, NE])
        ones = sb("ones", [P, DK])
        probs_even = sb("probs_even", [P, 2, TT, S])
        probs = [probs_even[:], x_tok[:].rearrange("p t d -> p (t d)").rearrange("p (h t s) -> p h t s", h=2, t=TT)]
        w_raw = acc[:].rearrange("p b s -> p (b s)").rearrange("p (w n) -> p w n", w=4)
        acc_half = acc[:, B // 2:].rearrange("p b s -> p (b s)")
        w1_raw = acc_half.rearrange("p (e f) -> p e f", e=NE)
        w2_raw = acc_half.rearrange("p (e c d) -> p e c d", e=NE, c=FC)
        wqk_cur = [sb(f"wqk_cur{j}", [P, 2, 2, P], F32R) for j in range(2)]
        wo_cur = sb("wo_cur", [P, 2, P], F32R)
        xT_cur = sb("xT_cur", [P, 2, S], F32R)
        q_pair, k_pair = (sb(n, [P, 2, S], F32R) for n in ("q_pair", "k_pair"))
        q_stack = [sb(f"q_stack{j}", [P, 2, 2, S], F32R) for j in range(2)]
        k_stack = [sb(f"k_stack{j}", [P, 2, 2, S], F32R) for j in range(2)]
        MAX_ROW = 96
        max_row = [[q_stack[j][MAX_ROW:MAX_ROW + TT, h, 1, 0:P] for h in range(2)] for j in range(2)]
        neg_max = [sb(f"neg_max{h}", [P, TT], F32R) for h in range(2)]
        v = sb("v", [P, 2, TT, 2, DK])
        probs_sum = [sb(f"probs_sum{h}", [P, S]) for h in range(2)]
        zT = sb("zT", [P, S])
        zT_hi, zT_lo = (sb(n, [P, S], F32R) for n in ("zT_hi", "zT_lo"))

        psum = ctx.enter_context(nc.psum_tensor("psum", [P, 8, 512], F32))
        COARSE, MISC, Z = 4, 6, 7

        g_hi = [stack[j][:, 0] for stack in (q_stack, k_stack) for j in range(2)]
        g_lo = [stack[j][:, 1] for stack in (q_stack, k_stack) for j in range(2)]
        GB = len(g_hi)
        silu = [probs[1][:, 0, FC * j:FC * (j + 1), :] for j in range(2)]
        gated = [probs[1][:, 1, FC * j:FC * (j + 1), :] for j in range(2)]
        gate_tab = wqk_cur[0][:, 0]
        cT = xT_cur
        CLO = 32
        select_e = k_pair[:].rearrange("p a s -> p (a s)").rearrange("p (e m) -> p e m", e=NE)
        logitT, sumT = (v[:, j].rearrange("p t h v -> p (t h v)") for j in range(2))
        free, carved = probs_even[:].rearrange("p h t s -> p (h t s)"), [0]

        def carve(*shape):
            n = 1
            for d in shape:
                n *= d
            ap = free[:, carved[0]:carved[0] + n]
            carved[0] += n
            names = " ".join("abc"[:len(shape)])
            return ap.rearrange(f"p ({names}) -> p {names}", **dict(zip("abc", shape))) if len(shape) > 1 else ap

        select_raw = carve(NE, P)
        exponent = carve(TT)
        before = carve(NE, NE)
        accT_cur = carve(S)
        x1_tok = carve(TT, D)
        out_tok = carve(TT, D)
        stats, stats2 = carve(TT, 6), carve(TT, 6)
        mv, mv2 = carve(TT, 2), carve(TT, 2)
        veps, veps2, rstd, rstd2, top, wsum, rwsum = (carve(TT) for _ in range(7))
        logit, shifted, expl, chosen, weight, combine = (carve(TT, NE) for _ in range(6))
        above, tied = carve(TT, NE, NE), carve(TT, NE, NE)
        assert carved[0] <= 2 * TT * S
        CB, Y, NA, NB = 4, 5, 6, 7

        def na(b):
            return COARSE if is_first(b) else NA

        def nb(b):
            return COARSE + 1 if is_first(b) else NB

        names = """x0_in x_near_in x_far_in w_in ident_set ones_set zeroed w_split
            xT_done xT_hi_done xT_lo_done acc_set acc_half acc_late
            wo_cur_in xT_cur_in
            q_done k_done vT_done q_hi_done q_lo_done k_hi_done k_lo_done v_done
            coarse_done max_done maxT_done max_row_done
            scores_done exp_done added pv_done sums_done sums_out z_done r_done
            zT_hi_done zT_lo_done wo_done acc_done
            experts_in x_out xt_cleared gate_in gate_set experts_hi experts_split sel_set const_set
            accT_in tok_done mv_done rstd_done x1_done x1T_done x1T_hi_done x1T_lo_done
            logitT_done logitT_out logit_done logit_out shifted route_step exp_logit c_done cT_done cT_hi_done cT_lo_done
            h_done cb_done silu_done gated g_hi_done g_lo_done y_done
            sum_half sum_done sum_tok_done mv2_done rstd2_done stats_done stats2_done norm2_done""".split()
        s = {n: sem(n) for n in names}
        q_stacked, k_stacked = ([[sem(f"{n}_stacked{j}{h}") for h in range(2)] for j in range(2)] for n in "qk")
        wqk_cur_in = [sem(f"wqk_cur_in{j}") for j in range(2)]
        shift_in = [sem(f"shift_in{h}") for h in range(2)]
        w_sem = [sem(f"w_in{k}") for k in range(4)]

        def wait(eng, semaphore, value):
            if not isinstance(value, int) or value > 0:
                eng.wait_ge(semaphore, value)

        def wait_apart(eng, *pairs):
            pairs = [(semaphore, v if isinstance(v, int) else eng.to_reg(v)) for semaphore, v in pairs]
            if not all(isinstance(v, int) for _, v in pairs):
                eng.wait_ge(s["ident_set"], 1)
            for semaphore, v in pairs:
                wait(eng, semaphore, v)

        def bits(ap):
            return ap.bitcast(F32)

        def loops(eng, body):
            for n in range(PEELED):
                body(n, n % 2)
            with eng.Fori(PEELED // 2, PAIRS // 2 - 1) as i:
                body(i * 2, 0)
                body(i * 2 + 1, 1)
            body(PAIRS - 2, 0)
            body(PAIRS - 1, 1)

        def chunks(eng, body):
            body(0, 0)
            body(1, 1)
            with eng.Fori(1, B // 2 - 1) as i:
                body(i * 2, 0)
                body(i * 2 + 1, 1)
            body(B - 2, 0)
            body(B - 1, 1)

        def late_sequences(n):
            if isinstance(n, int) and n in (PEELED - 2, PEELED - 1):
                return range(B // 2 + (n - PEELED + 2) * B // 4, B // 2 + (n - PEELED + 3) * B // 4)
            return ()

        def expert_quarter(step):
            half = slice(step % 2 * NE // 2, (step % 2 + 1) * NE // 2)
            if step < 2:
                return w1_tab[:, half, 1], w1_tab[:, half, 0], w1_raw[:, half]
            return w2_tab[:, half, :, 1], w2_tab[:, half, :, 0], w2_raw[:, half]

        def is_first(n):
            return isinstance(n, int) and n == 0

        def past(b, ahead):
            return isinstance(b, int) and b + ahead >= B

        def last_step(b, ahead):
            return isinstance(b, int) and b == B - 1 and ahead >= NE

        def is_last(n, ahead):
            return isinstance(n, int) and n + ahead >= PAIRS

        x_dram = x.rearrange("b (t p) d -> p (b t) d", p=P)
        w1_dram = w1.rearrange("e d f -> d e f")
        w2_dram = w2.rearrange("e (c p) d -> p e c d", p=P)
        w_dram = [w.rearrange("h d k -> d h k") for w in (w_q, w_k, w_v)]
        out_dram = out.rearrange("b (t p) d -> p (b t) d", p=P)

        block = ctx.enter_context(nc.Block())

        @block.sync
        def _(sp):
            def load_x(b):
                sp.dma_start(x_tok[:, b * TT:(b + 1) * TT, :], x_dram[:, b * TT:(b + 1) * TT, :]
                             ).then_inc(s["x0_in" if b == 0 else "x_near_in" if b < B // 2 else "x_far_in"], DMA)

            def load_w(k):
                sp.dma_start(w_raw[:, k, :].rearrange("p (h k) -> p h k", h=H), w_dram[k]).then_inc(w_sem[k], DMA)

            load_x(0)
            load_w(0)
            load_w(1)
            for b in range(1, B // 2):
                load_x(b)

            def load_wqk(m, j):
                if not (isinstance(m, int) and m < 4):
                    wait_apart(sp, (s["k_done"], m - 1))
                sp.dma_start(bits(wqk_cur[j][:]), bits(w_tab[:, m % HP, 0:2])).then_inc(wqk_cur_in[j], DMA)

            def load_xT(m):
                wait_apart(sp, (s["vT_done"], m // 2))
                sp.dma_start(bits(xT_cur[:]), bits(xT[:, m // HP])).then_inc(s["xT_cur_in"], DMA)

            def stack_q(j, m, h):
                wait_apart(sp, (s["scores_done"], 4 * (m - 2) + 2 * h + 2), (s["q_hi_done"], m + 1), (s["q_lo_done"], m + 1))
                half = slice(h * DK, (h + 1) * DK)
                sp.dma_start(bits(q_stack[j][0:DK, h]), bits(q_pair[half])).then_inc(q_stacked[j][h], DMA)
                sp.dma_start(bits(q_stack[j][DK:P, h, 0]), bits(q_pair[half, 0])).then_inc(q_stacked[j][h], DMA)

            def stack_k(j, m, h):
                wait_apart(sp, (s["scores_done"], 4 * (m - 2) + 2 * h + 2), (s["k_hi_done"], m + 1), (s["k_lo_done"], m + 1))
                half = slice(h * DK, (h + 1) * DK)
                sp.dma_start(bits(k_stack[j][0:DK, h]),
                             bits(k_pair[half, 0:1]).broadcast_to([DK, 2, S])).then_inc(k_stacked[j][h], DMA)
                sp.dma_start(bits(k_stack[j][DK:P, h, 0]), bits(k_pair[half, 1])).then_inc(k_stacked[j][h], DMA)

            def load_shift(j, h, k):
                wait(sp, s["max_row_done"], k + 1)
                sp.dma_start(bits(q_stack[j][DK:EXT, h, 1, :]), bits(max_row[j][h])).then_inc(shift_in[h], DMA)

            for h in range(2):
                stack_q(0, 0, h)
            load_w(2)
            for h in range(2):
                stack_k(0, 0, h)
            sp.dma_start(w_raw[:, 3, :].rearrange("p (c d) -> p c d", c=HP),
                         w_o.rearrange("(c p) d -> p c d", p=P)).then_inc(w_sem[3], DMA)
            for b in range(B // 2, B):
                load_x(b)
            for h in range(2):
                stack_q(1, 1, h)
            for h in range(2):
                stack_k(1, 1, h)
            sp.dma_start(gate_raw[:], gate_w).then_inc(s["gate_in"], DMA)
            sp.wait_ge(s["w_split"], 2)
            load_wqk(2, 0)
            sp.wait_ge(s["xT_hi_done"], 1)
            sp.wait_ge(s["xT_lo_done"], 1)
            load_xT(0)
            load_shift(0, 0, 0)

            def load_wo(m):
                wait_apart(sp, (s["wo_done"], m))
                sp.dma_start(bits(wo_cur[:]), bits(w_tab[:, m % HP, 3])).then_inc(s["wo_cur_in"], DMA)

            def body(n, j):
                if isinstance(n, int) and n == 1:
                    sp.wait_ge(s["w_split"], 4)
                    sp.wait_ge(s["xT_hi_done"], B)
                    sp.wait_ge(s["xT_lo_done"], B)
                    sp.dma_start(w1_raw, w1_dram).then_inc(s["experts_in"], DMA)
                if isinstance(n, int) and n == SPLIT_AT[2]:
                    sp.wait_ge(s["experts_split"], 2)
                    sp.dma_start(w2_raw, w2_dram).then_inc(s["experts_in"], DMA)
                if j == 0 and not is_first(n):
                    load_xT(n)
                load_shift(j, 1, 2 * n + 1)
                if not is_last(n, 2):
                    stack_q(j, n + 2, 0)
                if not is_last(n, 3):
                    load_wqk(n + 3, 1 - j)
                if not is_last(n, 1):
                    load_shift(1 - j, 0, 2 * n + 2)
                if not is_last(n, 2):
                    stack_q(j, n + 2, 1)
                    stack_k(j, n + 2, 0)
                if not is_first(n):
                    load_wo(n - 1)
                if not is_last(n, 2):
                    stack_k(j, n + 2, 1)

            loops(sp, body)

            def load_accT(b):
                wait_apart(sp, (s["tok_done"], b))
                sp.dma_start(accT_cur[:], acc[:, b, :]).then_inc(s["accT_in"], DMA)

            def store(b):
                wait_apart(sp, (s["norm2_done"], TT * (b + 1)))
                sp.dma_start(out_dram[:, bass.ds(b * TT, TT), :], out_tok).then_inc(s["x_out"], DMA)

            sp.wait_ge(s["pv_done"], PAIRS - 1)
            sp.wait_ge(s["added"], 2 * (TT - 1) * (PAIRS - 1))
            sp.wait_ge(s["acc_done"], HP)
            load_accT(0)
            load_wo(PAIRS - 1)
            sp.wait_ge(s["acc_done"], 2 * HP)
            load_accT(1)
            sp.wait_ge(s["acc_done"], PAIRS)

            def chunk(b, j):
                if not past(b, 2):
                    load_accT(b + 2)
                if not is_first(b):
                    store(b - 1)

            chunks(sp, chunk)
            store(B - 1)
            sp.wait_ge(s["x_out"], DMA * B)

        @block.gpsimd
        def _(pool):
            nc.gpsimd.memset(ident[:], 0.0).then_inc(s["zeroed"], 1)
            pool.wait_ge(s["zeroed"], 1)
            nc.gpsimd.affine_select(out=ident[:], in_=ident[:], compare_op=ALU.not_equal, fill=1.0, base=0,
                                    pattern=[[-1, P]], channel_multiplier=1).then_inc(s["ident_set"], 1)
            pool.wait_ge(s["ident_set"], 1)
            nc.gpsimd.memset(ones[:], 1.0).then_inc(s["ones_set"], 1)
            for j in range(2):
                pool.wait_ge(s["ones_set"], j + 1)
                nc.gpsimd.memset(bits(k_stack[j][DK:EXT, :, 1, :]), 1.0).then_inc(s["ones_set"], 1)
            pool.wait_ge(s["ones_set"], 3)

            def add_probs(n, j, h):
                wait(pool, s["sums_done"], n)
                for c in range(1, TT):
                    pool.wait_ge(s["exp_done"], 4 * n + 2 * h + (1 if c == 1 else 2))
                    if c > 1:
                        pool.wait_ge(s["added"], (TT - 1) * (2 * n + h) + c - 1)
                    left = probs[j][:, h, 0, :] if c == 1 else probs_sum[h][:]
                    nc.gpsimd.tensor_tensor(probs_sum[h][:], left, probs[j][:, h, c, :], ALU.add).then_inc(s["added"], 1)

            def body(n, j):
                if not is_first(n):
                    add_probs(n - 1, 1 - j, 1)
                add_probs(n, j, 0)
                if isinstance(n, int) and n - 1 in SPLIT_AT:
                    expert_lo(SPLIT_AT.index(n - 1))

            def expert_lo(step):
                lo, hi, raw = expert_quarter(step)
                pool.wait_ge(s["experts_hi"], step + 1)
                nc.gpsimd.tensor_tensor(lo, raw, bits(hi), ALU.subtract).then_inc(s["experts_split"], 1)

            loops(pool, body)
            pool.wait_ge(s["k_done"], PAIRS)
            nc.gpsimd.memset(bits(gate_tab), 0.0).then_inc(s["gate_set"], 1)
            add_probs(PAIRS - 1, 1, 1)

            def rstd_part(sem_in, sem_out, mvs, v, r, b):
                wait_apart(pool, (s[sem_in], TT * (b + 1)))
                nc.gpsimd.tensor_scalar(v[:], mvs[:, :, 1], 1.0, EPS, ALU.mult, ALU.add).then_inc(s[sem_out], 1)
                pool.wait_ge(s[sem_out], 2 * b + 1)
                nc.gpsimd.tensor_tensor(r[:], v[:], exponent, ALU.pow).then_inc(s[sem_out], 1)

            def g_lo_part(k, e):
                pool.wait_ge(s["g_hi_done"], k + 1)
                nc.gpsimd.tensor_tensor(g_lo[e % GB], gated[e % 2], bits(g_hi[e % GB]), ALU.subtract).then_inc(s["g_lo_done"], 1)

            pool.wait_ge(s["pv_done"], PAIRS - 1)
            nc.gpsimd.memset(exponent, -0.5).then_inc(s["const_set"], 1)
            pool.wait_ge(s["const_set"], 1)
            rstd_part("mv_done", "rstd_done", mv, veps, rstd, 0)
            nc.gpsimd.memset(before, 0.0).then_inc(s["const_set"], 1)
            pool.wait_ge(s["const_set"], 2)
            nc.gpsimd.affine_select(out=before, in_=before, compare_op=ALU.is_ge, fill=1.0, base=0,
                                    pattern=[[-1, NE], [1, NE]], channel_multiplier=0).then_inc(s["const_set"], 1)
            nc.gpsimd.memset(select_raw, 0.0).then_inc(s["sel_set"], 1)
            pool.wait_ge(s["sel_set"], 1)
            for i, first in enumerate((0, CLO)):
                nc.gpsimd.affine_select(out=select_raw, in_=select_raw, compare_op=ALU.not_equal, fill=1.0,
                                        base=-first, pattern=[[-1, NE], [0, P]], channel_multiplier=1).then_inc(s["sel_set"], 1)
                pool.wait_ge(s["sel_set"], i + 2)
            pool.wait_ge(s["scores_done"], 4 * PAIRS)
            nc.gpsimd.tensor_scalar(select_e, select_raw, 1.0, 0.0, ALU.mult, ALU.add).then_inc(s["sel_set"], 1)
            nc.gpsimd.memset(bits(cT[:]), 0.0).then_inc(s["xt_cleared"], 1)
            rstd_part("mv_done", "rstd_done", mv, veps, rstd, 1)
            g_lo_part(0, 0)
            g_lo_part(1, 1)

            def chunk(b, j):
                for e in range(NE):
                    if not last_step(b, e + 2):
                        g_lo_part(b * NE + e + 2, (e + 2) % NE)
                    if e == 3 and not is_first(b):
                        rstd_part("mv2_done", "rstd2_done", mv2, veps2, rstd2, b - 1)
                    if e == 5 and not past(b, 2):
                        rstd_part("mv_done", "rstd_done", mv, veps, rstd, b + 2)

            chunks(pool, chunk)
            rstd_part("mv2_done", "rstd2_done", mv2, veps2, rstd2, B - 1)

        @block.tensor
        def _(pe):
            def transpose_x(b):
                wait(pe, s["acc_set"], b - 3)
                for t in range(TT):
                    mm = nc.tensor.transpose(psum[:, b % 4, t * P:(t + 1) * P], x_tok[:, b * TT + t, :], ident[:])
                mm.then_inc(s["xT_done"], 1)

            def product(dst, left, right, start=True, stop=True):
                (lh, ll), (rh, rl) = left, right
                nc.tensor.matmul(dst, lh, rh, start=start, stop=False)
                nc.tensor.matmul(dst, lh, rl, start=False, stop=False)
                return nc.tensor.matmul(dst, ll, rh, start=False, stop=stop)

            def project_qk(which, m, j):
                first = isinstance(m, int) and m < 2
                w = [w_tab[:, m, which, part, :] if first else wqk_cur[j][:, which, part, :] for part in range(2)]
                return product(psum[:, MISC, :], w, [xT[:, m // HP, part, :] for part in range(2)])

            def project_q(m, i, j):
                if isinstance(m, int) and m < 2:
                    pe.wait_ge(s["w_split"], 1)
                else:
                    pe.wait_ge(wqk_cur_in[j], DMA * i)
                wait(pe, s["k_hi_done"], m)
                wait(pe, s["k_lo_done"], m)
                project_qk(0, m, j).then_inc(s["q_done"], 1)

            def project_k(m, j):
                if isinstance(m, int) and m < 2:
                    pe.wait_ge(s["w_split"], 2)
                pe.wait_ge(s["q_hi_done"], m + 1)
                pe.wait_ge(s["q_lo_done"], m + 1)
                wait(pe, s["sums_out"], m - 2)
                project_qk(1, m, j).then_inc(s["k_done"], 1)

            def project_v(m):
                pe.wait_ge(s["xT_cur_in"], DMA * (m // 2 + 1))
                pe.wait_ge(s["exp_done"], 4 * m + 4)
                for t in range(TT):
                    tok = slice(t * P, (t + 1) * P)
                    mm = product(psum[:, 2 + t // 2, t % 2 * 2 * P:(t % 2 + 1) * 2 * P], [xT_cur[:, part, tok] for part in range(2)],
                                 [w_tab[:, bass.ds(m % HP, 2), 2, part, :] for part in range(2)])
                mm.then_inc(s["vT_done"], 1)

            def coarse(n, i, j, h, t):
                k = 2 * n + h
                if t == 0:
                    pe.wait_ge(q_stacked[j][h], STACK * (i + 1))
                    pe.wait_ge(k_stacked[j][h], STACK * (i + 1))
                wait(pe, s["max_done"], TT * k + t - 1)
                if t == 1:
                    wait(pe, s["max_row_done"], k)
                nc.tensor.matmul(psum[:, COARSE + t % 2, :], q_stack[j][:, h, 0, t * P:(t + 1) * P], k_stack[j][:, h, 0, :],
                                 start=True, stop=True).then_inc(s["coarse_done"], 1)

            def shift_rows(n, h):
                k = 2 * n + h
                pe.wait_ge(s["max_done"], TT * (k + 1))
                nc.tensor.transpose(psum[0:TT, COARSE + 1, 0:P], bits(neg_max[h][:]), ident[:]).then_inc(s["maxT_done"], 1)

            def scores(n, j, h, groups=range(2)):
                k = 2 * n + h
                if groups[0] == 0:
                    pe.wait_ge(shift_in[h], DMA * (n + 1))
                if is_first(n):
                    pe.wait_ge(s["xT_lo_done"], B)
                for g in groups:
                    wait(pe, s["exp_done"], 2 * (k - 1) + g + 1)
                    if j == 1 and h == 0 and g == 1:
                        pe.wait_ge(s["v_done"], (n - 1) // 2 + 1)
                    for t in range(2 * g, 2 * g + 2):
                        keys = slice(t * P, (t + 1) * P)
                        nc.tensor.matmul(psum[:, t, :], k_stack[j][:, h, 0, keys], q_stack[j][:, h, 0, :], start=True, stop=False)
                        mm = nc.tensor.matmul(psum[:, t, :], k_stack[j][0:EXT, h, 1, keys], q_stack[j][0:EXT, h, 1, :], start=False, stop=True)
                    mm.then_inc(s["scores_done"], 1)

            def times_v(n, j, c):
                if c == 0:
                    pe.wait_ge(s["exp_done"], 4 * n + 4)
                    pe.wait_ge(s["v_done"], (n - j) // 2 + 1)
                    wait(pe, s["z_done"], n)
                for h in range(2):
                    mm = nc.tensor.matmul(psum[h * DK:(h + 1) * DK, Z, :], v[:, j, c, h, :], probs[j][:, h, c, :],
                                          start=(c == 0), stop=(c == TT - 1))
                if c == TT - 1:
                    mm.then_inc(s["pv_done"], 1)

            def sum_probs(n, j):
                pe.wait_ge(s["added"], (TT - 1) * 2 * (n + 1))
                pe.wait_ge(s["q_hi_done"], n + 4 if not is_last(n, 3) else PAIRS)
                pe.wait_ge(s["q_lo_done"], n + 4 if not is_last(n, 3) else PAIRS)
                if is_last(n, 1):
                    pe.wait_ge(s["acc_done"], n - 1)
                for h in range(2):
                    mm = nc.tensor.matmul(psum[h * DK:(h + 1) * DK, MISC, :], ones[:], probs_sum[h][:], start=True, stop=True)
                mm.then_inc(s["sums_done"], 1)

            def project_out(n):
                pe.wait_ge(s["zT_hi_done"], n + 1)
                pe.wait_ge(s["zT_lo_done"], n + 1)
                pe.wait_ge(s["wo_cur_in"], DMA * (n + 1))
                pe.wait_ge(s["k_hi_done"], n + 5 if not is_last(n, 4) else PAIRS)
                pe.wait_ge(s["k_lo_done"], n + 5 if not is_last(n, 4) else PAIRS)
                pe.wait_ge(s["sums_out"], n + 2 if not is_last(n, 1) else PAIRS)
                if is_last(n, 1):
                    pe.wait_ge(s["acc_done"], n)
                mm = product(psum[:, MISC, :], [wo_cur[:, 0, :], wo_cur[:, 1, :]], [zT_hi[:], zT_lo[:]])
                mm.then_inc(s["wo_done"], 1)

            pe.wait_ge(s["ident_set"], 1)
            pe.wait_ge(s["x0_in"], DMA)
            transpose_x(0)
            pe.wait_ge(s["xT_hi_done"], 1)
            pe.wait_ge(s["xT_lo_done"], 1)
            project_q(0, 0, 0)
            pe.wait_ge(s["x_near_in"], DMA * (B // 2 - 1))
            transpose_x(1)
            project_k(0, 0)
            transpose_x(2)
            project_q(1, 0, 1)
            transpose_x(3)
            project_k(1, 1)
            pe.wait_ge(s["ones_set"], 3)
            for h in range(2):
                for t in range(TT):
                    coarse(0, 0, 0, h, t)
                if h == 0:
                    shift_rows(0, 0)
            pe.wait_ge(s["x_far_in"], DMA * (B // 2))
            for b in range(B // 2, B):
                transpose_x(b)

            def body(n, j):
                ahead, project = not is_last(n, 1), not is_last(n, 2)

                def turn(m, parity):
                    return (m - parity) // 2

                former, before_former = not is_first(n), not (isinstance(n, int) and n < 2)

                def next_coarse(h, t):
                    if ahead:
                        coarse(n + 1, turn(n + 1, 1 - j), 1 - j, h, t)

                scores(n, j, 0)
                shift_rows(n, 1)
                next_coarse(0, 0)
                if project:
                    project_q(n + 2, turn(n + 2, j), j)
                next_coarse(0, 1)
                if former:
                    times_v(n - 1, 1 - j, 0)
                next_coarse(0, 2)
                if former:
                    times_v(n - 1, 1 - j, 1)
                    sum_probs(n - 1, 1 - j)
                next_coarse(0, 3)
                scores(n, j, 1, (0,))
                if ahead:
                    shift_rows(n + 1, 0)
                if project:
                    project_k(n + 2, j)
                scores(n, j, 1, (1,))
                next_coarse(1, 0)
                if former:
                    times_v(n - 1, 1 - j, 2)
                if before_former:
                    project_out(n - 2)
                next_coarse(1, 1)
                if j == 0:
                    project_v(n)
                next_coarse(1, 2)
                if former:
                    times_v(n - 1, 1 - j, 3)
                next_coarse(1, 3)

            loops(pe, body)
            def to_tokens(b):
                pe.wait_ge(s["accT_in"], DMA * (b + 1))
                if isinstance(b, int) and b == 1:
                    pe.wait_ge(s["acc_done"], PAIRS)
                else:
                    wait(pe, s["cT_hi_done"], b)
                    wait(pe, s["cT_lo_done"], b)
                for t in range(TT):
                    mm = nc.tensor.transpose(psum[:, na(b), t * P:(t + 1) * P], accT_cur[:, t * P:(t + 1) * P], ident[:])
                mm.then_inc(s["tok_done"], 1)

            def transpose_x1(b):
                pe.wait_ge(s["x1_done"], TT * (b + 1))
                for t in range(TT):
                    mm = nc.tensor.transpose(psum[:, na(b), t * P:(t + 1) * P], x1_tok[:, t, :], ident[:])
                mm.then_inc(s["x1T_done"], 1)

            def route(b):
                pe.wait_ge(s["x1T_hi_done"], b + 1)
                pe.wait_ge(s["x1T_lo_done"], b + 1)
                wait(pe, s["norm2_done"], TT * (b - 2))
                product(psum[:, nb(b), :], [gate_tab[:, 0, :], gate_tab[:, 1, :]],
                        [xT[:, b, 0, :], xT[:, b, 1, :]]).then_inc(s["logitT_done"], 1)

            def logits_to_tokens(b):
                pe.wait_ge(s["logitT_out"], b + 1)
                for t in range(TT):
                    mm = nc.tensor.transpose(psum[:, nb(b), t * P:(t + 1) * P], logitT[:, t * P:(t + 1) * P], ident[:])
                mm.then_inc(s["logit_done"], 1)

            def transpose_c(b):
                pe.wait_ge(s["c_done"], b + 1)
                for t in range(TT):
                    mm = nc.tensor.transpose(psum[0:NE, na(b), t * P:(t + 1) * P], combine[:, t, :], ident[:])
                mm.then_inc(s["cT_done"], 1)

            def hidden(k, b, e):
                wait(pe, s["silu_done"], k - 1)
                for f in range(FC):
                    cols = slice(f * P, (f + 1) * P)
                    mm = product(psum[:, FC * (e % 2) + f, :], [w1_tab[:, e, 0, cols], w1_tab[:, e, 1, cols]],
                                 [xT[:, b, 0, :], xT[:, b, 1, :]])
                mm.then_inc(s["h_done"], 1)

            def spread_c(k, b, j, e):
                if e == 0:
                    pe.wait_ge(s["cT_hi_done"], b + 1)
                    pe.wait_ge(s["cT_lo_done"], b + 1)
                wait(pe, s["gated"], k)
                nc.tensor.matmul(psum[:, CB, :], select_e[:, e, :], cT[:, j, :], start=True,
                                 stop=True).then_inc(s["cb_done"], 1)

            def second(k, b, e):
                if e == 0:
                    wait(pe, s["sum_half"], b)
                pe.wait_ge(s["g_hi_done"], k + 1)
                for f in range(FC):
                    for part in range(2):
                        nc.tensor.matmul(psum[:, Y, :], w2_tab[:, e, f, part, :], g_hi[e % GB][:, f, :],
                                         start=(e == 0 and f == 0 and part == 0), stop=False)
                pe.wait_ge(s["g_lo_done"], k + 1)
                for f in range(FC):
                    mm = nc.tensor.matmul(psum[:, Y, :], w2_tab[:, e, f, 0, :], g_lo[e % GB][:, f, :],
                                          start=False, stop=(e == NE - 1 and f == FC - 1))
                mm.then_inc(s["y_done"], 1)

            def sum_to_tokens(b):
                pe.wait_ge(s["sum_done"], b + 1)
                wait(pe, s["logit_out"], b + 3 if not past(b, 2) else B)
                for t in range(TT):
                    mm = nc.tensor.transpose(psum[:, NB, t * P:(t + 1) * P], sumT[:, t * P:(t + 1) * P], ident[:])
                mm.then_inc(s["sum_tok_done"], 1)

            to_tokens(0)
            sum_probs(PAIRS - 1, 1)
            for c in range(2):
                times_v(PAIRS - 1, 1, c)
            transpose_x1(0)
            for c in range(2, TT):
                times_v(PAIRS - 1, 1, c)
            project_out(PAIRS - 2)
            pe.wait_ge(s["gate_set"], 3)
            route(0)
            project_out(PAIRS - 1)
            logits_to_tokens(0)
            pe.wait_ge(s["experts_split"], 4)
            pe.wait_ge(s["exp_done"], 4 * PAIRS)
            hidden(0, 0, 0)
            hidden(1, 0, 1)
            to_tokens(1)
            transpose_c(0)
            pe.wait_ge(s["sel_set"], 4)
            spread_c(0, 0, 0, 0)
            transpose_x1(1)
            spread_c(1, 0, 0, 1)
            hidden(2, 0, 2)
            spread_c(2, 0, 0, 2)

            def chunk(b, j):
                for e in range(NE):
                    k = b * NE + e
                    if not last_step(b, e + 3):
                        hidden(k + 3, b + (e + 3) // NE, (e + 3) % NE)
                    if e > 0:
                        second(k, b, e)
                    if not last_step(b, e + 3):
                        spread_c(k + 3, b + (e + 3) // NE, (j + (e + 3) // NE) % 2, (e + 3) % NE)
                    if e == 0:
                        second(k, b, e)
                    if not past(b, 1):
                        if e == 0:
                            route(b + 1)
                        if e == 1:
                            logits_to_tokens(b + 1)
                        if e == 3:
                            transpose_c(b + 1)
                    if e == 2 and not is_first(b):
                        sum_to_tokens(b - 1)
                    if not past(b, 2):
                        if e == 4:
                            to_tokens(b + 2)
                        if e == 7:
                            transpose_x1(b + 2)

            chunks(pe, chunk)
            sum_to_tokens(B - 1)

        @block.scalar
        def _(act):
            def w_part(k):
                act.wait_ge(w_sem[k], DMA)
                nc.scalar.activation(w_tab[:, :, k, 0, :], w_raw[:, k, :].rearrange("p (c n) -> p c n", c=HP),
                                     ACT.Copy).then_inc(s["w_in"], 1)

            def xT_part(b):
                act.wait_ge(s["xT_done"], b + 1)
                nc.scalar.activation(xT[:, b, 0, :], psum[:, b % 4, :], ACT.Copy).then_inc(s["xT_hi_done"], 1)

            def double(b):
                act.wait_ge(s["xT_lo_done"], b + 1)
                act.wait_ge(s["w_split"], b * 4 // B + 1)
                nc.scalar.activation(acc[:, b, :], psum[:, b % 4, :], ACT.Copy, scale=2.0).then_inc(s["acc_set"], 1)

            def q_part(n, j):
                act.wait_ge(s["q_done"], n + 1)
                free_stage(q_stacked, n, j)
                nc.scalar.activation(q_pair[:, 0, :], psum[:, MISC, :], ACT.Copy, scale=SCALE).then_inc(s["q_hi_done"], 1)

            def k_part(n, j):
                act.wait_ge(s["k_done"], n + 1)
                free_stage(k_stacked, n, j)
                nc.scalar.activation(k_pair[:, 0, :], psum[:, MISC, :], ACT.Copy).then_inc(s["k_hi_done"], 1)

            def free_stage(stacked, n, j):
                for h in range(2):
                    wait(act, stacked[1 - j][h], STACK * ((n - 1 - (1 - j)) // 2 + 1))

            def v_part(m):
                act.wait_ge(s["vT_done"], m // 2 + 1)
                wait(act, s["pv_done"], m)
                nc.scalar.activation(v[:].rearrange("p j t h k -> p t j (h k)"),
                                     psum[:, 2:4, :].rearrange("p b (t j k) -> p (b t) j k", t=2, j=2),
                                     ACT.Copy).then_inc(s["v_done"], 1)

            def exps(n, j, h, groups=range(2)):
                k = 2 * n + h
                wait(act, s["pv_done"], n - 1)
                wait(act, s["sums_done"], n - 1)
                for g in groups:
                    act.wait_ge(s["scores_done"], 2 * k + g + 1)
                    nc.scalar.activation(probs[j][:, h, 2 * g:2 * g + 2, :], psum[:, 2 * g:2 * g + 2, :],
                                         ACT.Exp).then_inc(s["exp_done"], 1)

            def sums_part(n):
                act.wait_ge(s["sums_done"], n + 1)
                wait(act, s["zT_lo_done"], n)
                nc.scalar.activation(zT[:], psum[:, MISC, :], ACT.Copy).then_inc(s["sums_out"], 1)

            def zT_part(n):
                act.wait_ge(s["z_done"], n + 1)
                wait(act, s["wo_done"], n)
                nc.scalar.activation(zT_hi[:], zT[:], ACT.Copy).then_inc(s["zT_hi_done"], 1)

            xT_part(0)
            for k in range(2):
                w_part(k)
            q_part(0, 0)
            xT_part(1)
            k_part(0, 0)
            xT_part(2)
            double(0)
            q_part(1, 1)
            xT_part(3)
            double(1)
            k_part(1, 1)
            double(2)
            double(3)
            for k in range(2, 4):
                w_part(k)
            for b in range(B // 2, B):
                xT_part(b)

            def expert_hi(step):
                act.wait_ge(s["experts_in"], (step // 2 + 1) * DMA)
                lo, hi, raw = expert_quarter(step)
                nc.scalar.activation(hi, raw, ACT.Copy).then_inc(s["experts_hi"], 1)

            def double_late(b):
                act.wait_ge(s["experts_split"], 3 if b < 3 * B // 4 else 4)
                nc.scalar.activation(acc[:, b, :], bits(xT[:, b, 0, :]), ACT.Copy, scale=2.0).then_inc(s["acc_half"], 1)

            def body(n, j):
                exps(n, j, 0, (0,))
                if not (isinstance(n, int) and n < 2):
                    zT_part(n - 2)
                exps(n, j, 0, (1,))
                if not is_last(n, 2):
                    q_part(n + 2, j)
                if not is_first(n):
                    sums_part(n - 1)
                for b in late_sequences(n):
                    double_late(b)
                exps(n, j, 1, (0,))
                if not is_last(n, 2):
                    k_part(n + 2, j)
                exps(n, j, 1, (1,))
                if j == 0:
                    v_part(n)
                if isinstance(n, int) and n in SPLIT_AT:
                    expert_hi(SPLIT_AT.index(n))

            loops(act, body)
            def x1T_part(b):
                act.wait_ge(s["x1T_done"], b + 1)
                nc.scalar.activation(xT[:, b, 0, :], psum[:, na(b), :], ACT.Copy).then_inc(s["x1T_hi_done"], 1)

            def logitT_part(b):
                act.wait_ge(s["logitT_done"], b + 1)
                wait(act, s["logit_done"], b)
                nc.scalar.activation(logitT, psum[:, nb(b), :], ACT.Copy).then_inc(s["logitT_out"], 1)

            def exp_part(b):
                act.wait_ge(s["shifted"], b + 1)
                nc.scalar.activation(expl[:], shifted[:], ACT.Exp).then_inc(s["exp_logit"], 1)

            def cT_part(b, j):
                act.wait_ge(s["cT_done"], b + 1)
                wait(act, s["cb_done"], NE * (b - 1))
                nc.scalar.activation(cT[0:NE, j, :], psum[0:NE, na(b), :], ACT.Copy).then_inc(s["cT_hi_done"], 1)

            zT_part(PAIRS - 2)
            sums_part(PAIRS - 1)
            x1T_part(0)
            zT_part(PAIRS - 1)
            logitT_part(0)
            exp_part(0)

            def silu_part(k, e):
                act.wait_ge(s["h_done"], k + 1)
                wait(act, s["gated"], k - 1)
                nc.scalar.activation(silu[e % 2], psum[:, FC * (e % 2):FC * (e % 2 + 1), :],
                                     ACT.Silu).then_inc(s["silu_done"], 1)

            def g_hi_part(k, e):
                act.wait_ge(s["gated"], k + 1)
                wait(act, s["y_done"], k - GB + 1)
                nc.scalar.activation(g_hi[e % GB], gated[e % 2], ACT.Copy).then_inc(s["g_hi_done"], 1)

            act.wait_ge(s["xt_cleared"], 1)
            cT_part(0, 0)
            silu_part(0, 0)
            silu_part(1, 1)
            g_hi_part(0, 0)
            x1T_part(1)
            silu_part(2, 2)
            g_hi_part(1, 1)

            def chunk(b, j):
                for e in range(NE):
                    k = b * NE + e
                    if not last_step(b, e + 3):
                        silu_part(k + 3, (e + 3) % NE)
                    if not last_step(b, e + 2):
                        g_hi_part(k + 2, (e + 2) % NE)
                    if not past(b, 1):
                        if e == 0:
                            logitT_part(b + 1)
                        if e == 1:
                            exp_part(b + 1)
                        if e == 3:
                            cT_part(b + 1, 1 - j)
                    if e == 7 and not past(b, 2):
                        x1T_part(b + 2)

            chunks(act, chunk)

        @block.vector
        def _(dve):
            def w_part(k):
                dve.wait_ge(s["w_in"], k + 1)
                nc.vector.tensor_tensor(w_tab[:, :, k, 1, :], w_raw[:, k, :].rearrange("p (c n) -> p c n", c=HP),
                                        bits(w_tab[:, :, k, 0, :]), ALU.subtract).then_inc(s["w_split"], 1)

            def xT_part(b):
                dve.wait_ge(s["xT_hi_done"], b + 1)
                nc.vector.tensor_tensor(xT[:, b, 1, :], psum[:, b % 4, :], bits(xT[:, b, 0, :]),
                                        ALU.subtract).then_inc(s["xT_lo_done"], 1)

            def q_part(n, j):
                dve.wait_ge(s["q_hi_done"], n + 1)
                free_stage(q_stacked, n, j)
                nc.vector.scalar_tensor_tensor(q_pair[:, 1, :], psum[:, MISC, :], SCALE, bits(q_pair[:, 0, :]), ALU.mult,
                                               ALU.subtract).then_inc(s["q_lo_done"], 1)

            def k_part(n, j):
                dve.wait_ge(s["k_hi_done"], n + 1)
                free_stage(k_stacked, n, j)
                nc.vector.tensor_tensor(k_pair[:, 1, :], psum[:, MISC, :], bits(k_pair[:, 0, :]), ALU.subtract).then_inc(s["k_lo_done"], 1)

            def free_stage(stacked, n, j):
                for h in range(2):
                    wait(dve, stacked[1 - j][h], STACK * ((n - 1 - (1 - j)) // 2 + 1))

            def maxima(n, h, tiles=range(TT)):
                k = 2 * n + h
                if tiles[0] == 0:
                    wait(dve, s["maxT_done"], k - 1)
                for t in tiles:
                    dve.wait_ge(s["coarse_done"], TT * k + t + 1)
                    nc.vector.tensor_reduce(neg_max[h][:, t:t + 1], psum[:, COARSE + t % 2, :], AX.X, ALU.max,
                                            negate=True).then_inc(s["max_done"], 1)

            def shift_part(n, j, h):
                k = 2 * n + h
                dve.wait_ge(s["maxT_done"], k + 1)
                wait(dve, shift_in[h], DMA * n)
                nc.vector.tensor_copy(max_row[j][h], psum[0:TT, COARSE + 1, 0:P]).then_inc(s["max_row_done"], 1)

            def reciprocals(n, parts):
                dve.wait_ge(s["sums_out"], n + 1)
                for t in parts:
                    cols = slice(t * P, (t + 1) * P)
                    nc.vector.reciprocal(zT[:, cols], zT[:, cols]).then_inc(s["r_done"], 1)

            def z_part(n):
                dve.wait_ge(s["pv_done"], n + 1)
                dve.wait_ge(s["r_done"], TT * (n + 1))
                nc.vector.tensor_tensor(zT[:], psum[:, Z, :], zT[:], ALU.mult).then_inc(s["z_done"], 1)

            def zT_part(n):
                dve.wait_ge(s["zT_hi_done"], n + 1)
                wait(dve, s["wo_done"], n)
                nc.vector.tensor_tensor(zT_lo[:], zT[:], bits(zT_hi[:]), ALU.subtract).then_inc(s["zT_lo_done"], 1)

            def acc_part(n):
                dve.wait_ge(s["wo_done"], n + 1)
                wait(dve, s["acc_done"], n)
                if is_first(n):
                    dve.wait_ge(s["acc_set"], B // 2)
                if not isinstance(n, int):
                    dve.wait_ge(s["acc_late"], B // 2)
                a = acc[:, n // HP, :]
                nc.vector.tensor_tensor(a, psum[:, MISC, :], a, ALU.add).then_inc(s["acc_done"], 1)

            xT_part(0)
            for k in range(2):
                w_part(k)
            q_part(0, 0)
            xT_part(1)
            k_part(0, 0)
            xT_part(2)
            q_part(1, 1)
            xT_part(3)
            maxima(0, 0)
            shift_part(0, 0, 0)
            k_part(1, 1)
            maxima(0, 1)
            for k in range(2, 4):
                w_part(k)
            for b in range(B // 2, B):
                xT_part(b)

            def body(n, j):
                ahead, project, former = not is_last(n, 1), not is_last(n, 2), not is_first(n)

                def next_maximum(h, t):
                    if ahead:
                        maxima(n + 1, h, (t,))

                shift_part(n, j, 1)
                next_maximum(0, 0)
                if not (isinstance(n, int) and n < 2):
                    zT_part(n - 2)
                next_maximum(0, 1)
                if project:
                    q_part(n + 2, j)
                next_maximum(0, 2)
                next_maximum(0, 3)
                if former:
                    reciprocals(n - 1, (0,))
                if ahead:
                    shift_part(n + 1, 1 - j, 0)
                if former:
                    reciprocals(n - 1, (1,))
                if project:
                    k_part(n + 2, j)
                next_maximum(1, 0)
                if former:
                    reciprocals(n - 1, (2,))
                if not (isinstance(n, int) and n < 2):
                    acc_part(n - 2)
                next_maximum(1, 1)
                next_maximum(1, 2)
                if former:
                    reciprocals(n - 1, (3,))
                next_maximum(1, 3)
                if former:
                    z_part(n - 1)
                for b in late_sequences(n):
                    dve.wait_ge(s["acc_half"], b - B // 2 + 1)
                    nc.vector.scalar_tensor_tensor(acc[:, b, :], bits(xT[:, b, 1, :]), 2.0, acc[:, b, :], ALU.mult,
                                                   ALU.add).then_inc(s["acc_late"], 1)

            loops(dve, body)

            def norm_stats(bank, st, mvs, b, tok_sem, st_sem, mv_sem, free_sem):
                dve.wait_ge(s[tok_sem], b + 1)
                wait(dve, s[mv_sem], TT * b)
                for t in range(TT):
                    nc.vector.bn_stats(st[:, t], psum[:, bank, t * P:(t + 1) * P]).then_inc(s[st_sem], 1)
                wait_apart(dve, (s[st_sem], TT * (b + 1)), (s[free_sem[0]], free_sem[1] * b))
                for t in range(TT):
                    nc.vector.bn_aggr(mvs[:, t], st[:, t]).then_inc(s[mv_sem], 1)

            def stats1(b):
                norm_stats(na(b), stats, mv, b, "tok_done", "stats_done", "mv_done", ("x1_done", TT))

            def norm1(b):
                dve.wait_ge(s["rstd_done"], 2 * b + 2)
                wait(dve, s["x1T_done"], b)
                for t in range(TT):
                    nc.vector.tensor_scalar(x1_tok[:, t, :], psum[:, na(b), t * P:(t + 1) * P], mv[:, t, 0:1],
                                            rstd[:, t:t + 1], ALU.subtract, ALU.mult).then_inc(s["x1_done"], 1)

            def x1T_part(b):
                dve.wait_ge(s["x1T_hi_done"], b + 1)
                nc.vector.tensor_tensor(xT[:, b, 1, :], psum[:, na(b), :], bits(xT[:, b, 0, :]),
                                        ALU.subtract).then_inc(s["x1T_lo_done"], 1)

            def route1(b):
                dve.wait_ge(s["logit_done"], b + 1)
                wait(dve, s["c_done"], b)
                nc.vector.tensor_copy(logit[:], psum[:, nb(b), :].rearrange("p (t m) -> p t m", t=TT)[:, :, 0:NE]
                                      ).then_inc(s["logit_out"], 1)
                dve.wait_ge(s["logit_out"], b + 1)
                nc.vector.tensor_reduce(top[:], logit[:], AX.X, ALU.max).then_inc(s["route_step"], 1)
                dve.wait_ge(s["route_step"], ROUTE * b + 1)
                nc.vector.tensor_tensor(shifted[:], logit[:], over_experts(top), ALU.subtract).then_inc(s["shifted"], 1)
                other, own = logit[:].unsqueeze(2), logit[:].unsqueeze(3)
                shape = [P, TT, NE, NE]
                nc.vector.tensor_tensor(above[:], other.broadcast_to(shape), own.broadcast_to(shape),
                                        ALU.is_gt).then_inc(s["route_step"], 1)
                nc.vector.tensor_tensor(tied[:], other.broadcast_to(shape), own.broadcast_to(shape),
                                        ALU.is_equal).then_inc(s["route_step"], 1)
                dve.wait_ge(s["route_step"], ROUTE * b + 3)
                nc.vector.tensor_tensor(tied[:], tied[:], before.unsqueeze(1).broadcast_to(shape),
                                        ALU.mult).then_inc(s["route_step"], 1)
                dve.wait_ge(s["route_step"], ROUTE * b + 4)
                nc.vector.tensor_tensor(above[:], above[:], tied[:], ALU.add).then_inc(s["route_step"], 1)
                dve.wait_ge(s["route_step"], ROUTE * b + 5)
                nc.vector.tensor_reduce(chosen[:], above[:], AX.X, ALU.add).then_inc(s["route_step"], 1)

            def route2(b):
                dve.wait_ge(s["route_step"], ROUTE * b + 6)
                dve.wait_ge(s["exp_logit"], b + 1)
                nc.vector.scalar_tensor_tensor(weight[:], chosen[:], 2.0, expl[:], ALU.is_lt,
                                               ALU.mult).then_inc(s["route_step"], 1)
                dve.wait_ge(s["route_step"], ROUTE * b + 7)
                nc.vector.tensor_reduce(wsum[:], weight[:], AX.X, ALU.add).then_inc(s["route_step"], 1)
                dve.wait_ge(s["route_step"], ROUTE * b + 8)
                nc.vector.reciprocal(rwsum[:], wsum[:]).then_inc(s["route_step"], 1)
                dve.wait_ge(s["route_step"], ROUTE * b + 9)
                wait(dve, s["cT_done"], b)
                nc.vector.tensor_tensor(combine[:], weight[:], over_experts(rwsum), ALU.mult).then_inc(s["c_done"], 1)

            ROUTE = 9

            def over_experts(v):
                return v[:].unsqueeze(2).broadcast_to([P, TT, NE])

            def cT_part(b, j):
                dve.wait_ge(s["cT_hi_done"], b + 1)
                nc.vector.tensor_tensor(cT[CLO:CLO + NE, j, :], psum[0:NE, na(b), :], bits(cT[0:NE, j, :]),
                                        ALU.subtract).then_inc(s["cT_lo_done"], 1)

            zT_part(PAIRS - 2)
            dve.wait_ge(s["gate_in"], DMA)
            dve.wait_ge(s["gate_set"], 1)
            nc.vector.tensor_copy(gate_tab[:, 0, 0:NE], gate_raw[:]).then_inc(s["gate_set"], 1)
            dve.wait_ge(s["gate_set"], 2)
            nc.vector.tensor_tensor(gate_tab[:, 1, 0:NE], gate_raw[:], bits(gate_tab[:, 0, 0:NE]),
                                    ALU.subtract).then_inc(s["gate_set"], 1)
            stats1(0)
            norm1(0)
            reciprocals(PAIRS - 1, range(TT))
            x1T_part(0)
            z_part(PAIRS - 1)
            acc_part(PAIRS - 2)
            zT_part(PAIRS - 1)
            dve.wait_ge(s["const_set"], 3)
            acc_part(PAIRS - 1)
            route1(0)
            route2(0)
            stats1(1)

            def gate_part(k, e):
                dve.wait_ge(s["silu_done"], k + 1)
                dve.wait_ge(s["cb_done"], k + 1)
                wait(dve, s["g_lo_done"], k - 1)
                nc.vector.tensor_tensor(gated[e % 2], silu[e % 2],
                                        psum[:, CB, :].unsqueeze(1).broadcast_to([P, FC, S]),
                                        ALU.mult).then_inc(s["gated"], 1)

            def sum_part(b):
                dve.wait_ge(s["y_done"], NE * (b + 1))
                wait(dve, s["sum_tok_done"], b)
                nc.vector.tensor_tensor(sumT, psum[:, Y, :], bits(xT[:, b, 0, :]), ALU.add).then_inc(s["sum_half"], 1)
                dve.wait_ge(s["sum_half"], b + 1)
                nc.vector.tensor_tensor(sumT, sumT, bits(xT[:, b, 1, :]), ALU.add).then_inc(s["sum_done"], 1)

            def stats2_part(b):
                norm_stats(NB, stats2, mv2, b, "sum_tok_done", "stats2_done", "mv2_done", ("norm2_done", TT))

            def norm2(b):
                dve.wait_ge(s["rstd2_done"], 2 * b + 2)
                wait(dve, s["x_out"], DMA * b)
                for t in range(TT):
                    nc.vector.tensor_scalar(out_tok[:, t, :], psum[:, NB, t * P:(t + 1) * P], mv2[:, t, 0:1],
                                            rstd2[:, t:t + 1], ALU.subtract, ALU.mult).then_inc(s["norm2_done"], 1)

            dve.wait_ge(s["xt_cleared"], 1)
            cT_part(0, 0)
            gate_part(0, 0)
            norm1(1)
            gate_part(1, 1)
            x1T_part(1)
            gate_part(2, 2)

            def chunk(b, j):
                for e in range(NE):
                    if e == 0 and not is_first(b):
                        sum_part(b - 1)
                        if not past(b, 1):
                            x1T_part(b + 1)
                    if not last_step(b, e + 3):
                        gate_part(b * NE + e + 3, (e + 3) % NE)
                    if not past(b, 1):
                        if e == 1:
                            route1(b + 1)
                        if e == 2:
                            route2(b + 1)
                        if e == 3:
                            cT_part(b + 1, 1 - j)
                    if not is_first(b):
                        if e == 2:
                            stats2_part(b - 1)
                        if e == 4:
                            norm2(b - 1)
                    if not past(b, 2):
                        if e == 4:
                            stats1(b + 2)
                        if e == 6:
                            norm1(b + 2)

            chunks(dve, chunk)
            sum_part(B - 1)
            stats2_part(B - 1)
            norm2(B - 1)


_INS = ["L0_attn_x", "L0_attn_w_q", "L0_attn_w_k", "L0_attn_w_v", "L0_attn_w_o", "L0_ffn_gate_w", "L0_ffn_w1",
        "L0_ffn_w2"]


def kernel(**inputs):
    import numpy as np
    import concourse.bacc as bacc
    from concourse import mybir as mb
    from concourse.bass_utils import run_bass_kernel_spmd

    nc = bacc.Bacc("TRN2", target_bir_lowering=False, num_devices=1)
    arrays, args = {}, []
    for name in _INS:
        a = np.ascontiguousarray(inputs[name])
        arrays[f"{name}_dram"] = a
        args.append(nc.dram_tensor(f"{name}_dram", a.shape, mb.dt.from_np(a.dtype), kind="ExternalInput").ap())
    shape = inputs["L0_attn_x"].shape
    args.append(nc.dram_tensor("out_dram", shape, F32, kind="ExternalOutput").ap())
    attention_moe_kernel(nc, *args)
    r = run_bass_kernel_spmd(nc, [arrays], core_ids=[0])
    return r.results[0]["out_dram"]
```
